# Optimizing a Trainium2 kernel written in Bass

```python
import numpy as np
import jax
import jax.numpy as jnp

def _softmax(x, axis=-1):
    return jax.nn.softmax(x, axis=axis)
def _gelu(x):
    return jax.nn.gelu(x, approximate=True)
def _silu(x):
    return jax.nn.silu(x)
def _sigmoid(x):
    return jax.nn.sigmoid(x)
def _layernorm(x, axis=-1, eps=1e-5):
    m = jnp.mean(x, axis=axis, keepdims=True)
    v = jnp.var(x, axis=axis, keepdims=True)
    return (x - m) / jnp.sqrt(v + eps)
def _scatter_add(tgt, idx, src, axis=0):
    return tgt.at[idx].add(src)
def _segment_sum(src, seg, n):
    return jax.ops.segment_sum(src, seg, n)

kernel_name = 'mk_adj_preln_d4_adj_64_060e91'

def setup_inputs(seed: int = 0):
    np.random.seed(seed)
    _w = jnp.asarray
    def _rec_inputs():
        import jax
        import jax.numpy as jnp
        _gk = jax.random.key(seed)
        x = 0.0002141 + 1 * jax.random.normal(jax.random.fold_in(_gk, 1), (4096, 64), jnp.float32)
        _a = jax.random.bernoulli(jax.random.fold_in(_gk, 2), 0.000976562, (4096, 4096))
        _af = _a.astype(jnp.float32)
        adj = _af
        return x, adj
    x, adj = _rec_inputs()
    def _L0_gnn_setup():
        import jax, jax.numpy as jnp
        import numpy as np
        import math
        N = 12288
        D = 64
        SCALE0 = math.log(10.0)

        def lorentz_linear(x, W, b, scale):
            h = x @ W.T + b
            time = jax.nn.sigmoid(h[:, :1]) * jnp.exp(scale) + 1.1
            xn = h[:, 1:]
            sq = jnp.clip(jnp.sum(xn * xn, axis=-1, keepdims=True), 1e-08, None)
            s = (time * time - 1.0) / sq
            return jnp.concatenate([time, xn * jnp.sqrt(s)], axis=-1)
        key = jax.random.key(seed)
        ks = jax.random.split(key, 8)
        stdv = 1.0 / math.sqrt(D)
        x = jax.random.normal(ks[0], (N, D), dtype=jnp.float32)
        adj = (jax.random.uniform(ks[1], (N, N)) < 0.002).astype(jnp.float32)
        W = jax.random.uniform(ks[2], (D, D), minval=-stdv, maxval=stdv, dtype=jnp.float32)
        Wq = jax.random.uniform(ks[3], (D, D), minval=-stdv, maxval=stdv, dtype=jnp.float32)
        Wk = jax.random.uniform(ks[4], (D, D), minval=-stdv, maxval=stdv, dtype=jnp.float32)
        z = jnp.zeros((D,), dtype=jnp.float32)
        sc = jnp.asarray(SCALE0, dtype=jnp.float32)
        return {'x': x, 'adj': adj, 'W': W, 'b': z, 'scale': sc, 'Wq': Wq, 'bq': z, 'scale_q': sc, 'Wk': Wk, 'bk': z, 'scale_k': sc, 'att_bias': jnp.asarray(20.0, dtype=jnp.float32), 'att_scale': jnp.asarray(math.sqrt(D), dtype=jnp.float32)}
    _L0_gnn_all = _L0_gnn_setup()
    _L0_gnn_in = {k: v for k, v in _L0_gnn_all.items() if k in ('W', 'b', 'scale', 'Wq', 'bq', 'scale_q', 'Wk', 'bk', 'scale_k', 'att_bias', 'att_scale', )}
    del _L0_gnn_all

    def _L1_gnn_setup():
        import jax, jax.numpy as jnp
        import numpy as np
        N, D_IN, D_OUT = (8192, 64, 64)
        MAX_NEIGH = 100
        DECAY = 0.5
        key = jax.random.key(seed)
        k1, k2, k3, k4 = jax.random.split(key, 4)
        stdv = 1.0 / np.sqrt(D_OUT)
        inputs = {'input': jax.random.normal(k1, (N, D_IN), dtype=jnp.float32), 'adj': jax.random.randint(k2, (N, N), 0, 2).astype(jnp.float32), 'weight': jax.random.uniform(k3, (D_IN, D_OUT), minval=-stdv, maxval=stdv, dtype=jnp.float32), 'bias': jax.random.uniform(k4, (D_OUT,), minval=-stdv, maxval=stdv, dtype=jnp.float32)}
        return inputs
    _L1_gnn_all = _L1_gnn_setup()
    _L1_gnn_in = {k: v for k, v in _L1_gnn_all.items() if k in ('weight', 'bias', )}
    del _L1_gnn_all

    def _L2_gnn_setup():
        import jax, jax.numpy as jnp
        import numpy as np
        N = 10000
        DIM = 64
        F_CONST = 1.0
        B_CONST = 0.1
        R_CONST = 0.01
        key = jax.random.key(seed)
        k1, k2 = jax.random.split(key)
        t = jnp.zeros((1,), dtype=jnp.float32)
        x = jax.random.uniform(k1, (N, DIM), dtype=jnp.float32)
        A = jax.random.uniform(k2, (N, N), dtype=jnp.float32)
        return {'t': t, 'x': x, 'A': A}
    _L2_gnn_all = _L2_gnn_setup()
    _L2_gnn_in = {k: v for k, v in _L2_gnn_all.items() if k in ('t', )}
    del _L2_gnn_all

    def _L3_gnn_setup():
        import jax, jax.numpy as jnp
        import numpy as np
        N = 16384
        D_IN = 64
        D_OUT = 64
        EDGE_P = 0.002
        key = jax.random.key(seed)
        kx, ka, kw = jax.random.split(key, 3)
        X = jax.random.normal(kx, (N, D_IN), dtype=jnp.float32)
        adj = (jax.random.uniform(ka, (N, N)) < EDGE_P).astype(jnp.float32)
        W = jax.random.normal(kw, (D_OUT, 2 * D_IN), dtype=jnp.float32) * (1.0 / np.sqrt(2 * D_IN))
        return {'X': X, 'adj': adj, 'W': W}
    _L3_gnn_all = _L3_gnn_setup()
    _L3_gnn_in = {k: v for k, v in _L3_gnn_all.items() if k in ('W', )}
    del _L3_gnn_all

    return {
        "x": x,
        "adj": adj,
        "L0_gnn_W": _L0_gnn_in["W"],
        "L0_gnn_b": _L0_gnn_in["b"],
        "L0_gnn_scale": _L0_gnn_in["scale"],
        "L0_gnn_Wq": _L0_gnn_in["Wq"],
        "L0_gnn_bq": _L0_gnn_in["bq"],
        "L0_gnn_scale_q": _L0_gnn_in["scale_q"],
        "L0_gnn_Wk": _L0_gnn_in["Wk"],
        "L0_gnn_bk": _L0_gnn_in["bk"],
        "L0_gnn_scale_k": _L0_gnn_in["scale_k"],
        "L0_gnn_att_bias": _L0_gnn_in["att_bias"],
        "L0_gnn_att_scale": _L0_gnn_in["att_scale"],
        "L1_gnn_weight": _L1_gnn_in["weight"],
        "L1_gnn_bias": _L1_gnn_in["bias"],
        "L2_gnn_t": _L2_gnn_in["t"],
        "L3_gnn_W": _L3_gnn_in["W"],
    }

def reference(x, adj, L0_gnn_W, L0_gnn_b, L0_gnn_scale, L0_gnn_Wq, L0_gnn_bq, L0_gnn_scale_q, L0_gnn_Wk, L0_gnn_bk, L0_gnn_scale_k, L0_gnn_att_bias, L0_gnn_att_scale, L1_gnn_weight, L1_gnn_bias, L2_gnn_t, L3_gnn_W):
    import jax
    import jax.numpy as jnp
    def _L0_gnn_ref(x, adj, W, b, scale, Wq, bq, scale_q, Wk, bk, scale_k, att_bias, att_scale):
        import jax, jax.numpy as jnp
        import numpy as np
        import math
        N = 12288
        D = 64
        SCALE0 = math.log(10.0)

        def lorentz_linear(x, W, b, scale):
            h = x @ W.T + b
            time = jax.nn.sigmoid(h[:, :1]) * jnp.exp(scale) + 1.1
            xn = h[:, 1:]
            sq = jnp.clip(jnp.sum(xn * xn, axis=-1, keepdims=True), 1e-08, None)
            s = (time * time - 1.0) / sq
            return jnp.concatenate([time, xn * jnp.sqrt(s)], axis=-1)
        h = lorentz_linear(x, W, b, scale)
        q = lorentz_linear(h, Wq, bq, scale_q)
        k = lorentz_linear(h, Wk, bk, scale_k)
        qm = jnp.concatenate([-q[:, :1], q[:, 1:]], axis=-1)
        att = 2.0 + 2.0 * (qm @ k.T)
        att = jax.nn.sigmoid(att / att_scale + att_bias)
        att = adj * att
        support = att @ h
        inner = -support[:, :1] ** 2 + jnp.sum(support[:, 1:] ** 2, axis=-1, keepdims=True)
        denorm = jnp.sqrt(jnp.clip(jnp.abs(-inner), 1e-08, None))
        return support / denorm

    def _L1_gnn_ref(input, adj, weight, bias):
        import jax, jax.numpy as jnp
        import numpy as np
        N, D_IN, D_OUT = (8192, 64, 64)
        MAX_NEIGH = 100
        DECAY = 0.5
        support = input @ weight
        mask = (adj != 0).astype(support.dtype)
        rank = jnp.cumsum(mask, axis=1)
        deg = rank[:, -1:]
        k = jnp.minimum(deg, float(MAX_NEIGH))
        pos = rank - (deg - k)
        w = mask * jnp.where(pos > 0, DECAY ** (k - pos), 0.0)
        out = w @ support + bias
        return out

    def _L2_gnn_ref(t, x, A):
        import jax, jax.numpy as jnp
        import numpy as np
        N = 10000
        DIM = 64
        F_CONST = 1.0
        B_CONST = 0.1
        R_CONST = 0.01
        Ax = A @ x
        outer = R_CONST * jnp.sum(x * Ax, axis=1, keepdims=True)
        return F_CONST - B_CONST * x - outer

    def _L3_gnn_ref(X, adj, W):
        import jax, jax.numpy as jnp
        import numpy as np
        N = 16384
        D_IN = 64
        D_OUT = 64
        EDGE_P = 0.002
        deg = jnp.sum(adj, axis=1, keepdims=True)
        nb_agg = adj @ X / jnp.maximum(deg, 1.0)
        X_cat = jnp.concatenate([X, nb_agg], axis=1)
        out = X_cat @ W.T
        return jax.nn.relu(out)

    h = jnp.maximum(_layernorm(x, axis=-1), 0.0)
    x = x + _L0_gnn_ref(h, adj, L0_gnn_W, L0_gnn_b, L0_gnn_scale, L0_gnn_Wq, L0_gnn_bq, L0_gnn_scale_q, L0_gnn_Wk, L0_gnn_bk, L0_gnn_scale_k, L0_gnn_att_bias, L0_gnn_att_scale)
    h = jnp.maximum(_layernorm(x, axis=-1), 0.0)
    x = x + _L1_gnn_ref(h, adj, L1_gnn_weight, L1_gnn_bias)
    h = jnp.maximum(_layernorm(x, axis=-1), 0.0)
    x = x + _L2_gnn_ref(L2_gnn_t, h, adj)
    h = jnp.maximum(_layernorm(x, axis=-1), 0.0)
    x = x + _L3_gnn_ref(h, adj, L3_gnn_W)
    return x


_drawn_inputs = setup_inputs


def setup_inputs(seed=0):
    import zlib

    import numpy as np

    out = dict(_drawn_inputs(seed))
    spreads = {'L0_gnn_b': (0.0, 0.1), 'L0_gnn_bq': (0.0, 2.0), 'L0_gnn_bk': (0.0, 2.0)}
    factors = {'L0_gnn_Wq': 179.106, 'L0_gnn_Wk': 200.0}
    for name, (base, spread) in spreads.items():
        noise = np.random.default_rng([zlib.crc32(name.encode()), seed]).standard_normal(out[name].shape)
        drawn = base * np.exp(spread * noise) if base else spread * noise
        out[name] = jnp.asarray(drawn.astype(out[name].dtype))
    for name, factor in factors.items():
        out[name] = (out[name] * factor).astype(out[name].dtype)
    return out
```

```python
from contextlib import ExitStack

import concourse.bass as bass
from concourse import mybir

F32 = mybir.dt.float32
F16 = mybir.dt.float16
BF16 = mybir.dt.bfloat16
F8 = mybir.dt.float8e4
I32 = mybir.dt.int32
I16 = mybir.dt.int16
ALU = mybir.AluOpType
ACT = mybir.ActivationFunctionType
AX = mybir.AxisListType

P = 128
LO = 2.0 ** 11
CUT = 100
BIAS = 127
EPS = 1e-5
TINY = 1e-8
RSQRT_SEED = float(0x5F3759DF)
NC_ = P + 64 + 2


def gnn_program(nc, x_in, adj_in, w0_in, wqk_in, scalars_in, w1_in, bias1_in, w3h_in, w3n_in, consts_in, rank_in, out):
    N, D = x_in.shape
    T = N // P
    CH = 512
    CT = CH // P
    C = N // CH
    HALF = T // 2
    assert D == 64 and T == 32 and C == 8

    ctx = ExitStack()
    with ctx:
        def sb(name, shape, dt):
            return ctx.enter_context(nc.sbuf_tensor(name, shape, dt))

        def sem(name):
            return ctx.enter_context(nc.semaphore(name))

        adj8 = sb("adj8", [P, C, T, CH], F8)
        x = sb("x", [P, T, D], F32)
        feat = sb("feat", [P, T, D], F32)
        keys = sb("keys", [P, 2, N], F16)
        queries = sb("queries", [P, N], F16)
        att = sb("att", [P, 3, 2 * CH], F32)
        scratch = sb("scratch", [P, 5632], F32)
        consts = sb("consts", [P, NC_], F32)
        w0 = sb("w0", [D + 1, D], F32)
        wqk = sb("wqk", [D + 1, 2 * D], F32)
        c1 = sb("c1", [P, D], F32)
        c3 = sb("c3", [P, D], F32)
        w3h = sb("w3h", [D, D], F32)
        bias1 = sb("bias1", [1, D], F32)
        scal_row = sb("scal_row", [1, 5], F32)
        ones_row = sb("ones_row", [1, P], F32)
        scal = sb("scal", [P, 5], F32)
        exps = sb("exps", [P, 3], F32)
        zscale = sb("zscale", [P, 1], F32)
        zbias = sb("zbias", [P, 1], F32)
        ident16 = sb("ident16", [P, P], F16)
        rank_w = sb("rank_w", [P, P], BF16)
        carry_w = sb("carry_w", [P, P], BF16)
        st = sb("st", [P, 6, T], F32)
        stp = sb("stp", [P, 6, CT], F32)
        ident = consts[:, 0:P]
        c2 = consts[:, P:P + D]
        hilo1, hilo3 = consts[:, NC_ - 2:NC_ - 1], consts[:, NC_ - 1:NC_]

        GT = HALF
        QT = 8
        turned = scratch[:, 0:4096].rearrange("p (r n) -> p r n", r=2)
        pair_rows = scratch[:, 4096:5376].bitcast(F16).rearrange("p (t w) -> p t w", t=QT)
        rank_f32 = scratch[:, 4096:4352]
        pairs_a = scratch[:, 0:2048].bitcast(F16).rearrange("p (t w) -> p t w", t=T)
        sums = scratch[:, 2048:4096].rearrange("p (r n) -> p r n", r=4)
        ysb = scratch[:, 4096:5120].rearrange("p (r t d) -> p r t d", r=4, t=CT)
        tmp_p = scratch[:, 5120:5632].rearrange("p (r t d) -> p r t d", r=2, t=CT)
        pairs_b = queries[:, :].rearrange("p (t w) -> p t w", t=T)
        rdeg = keys[:, :, :].rearrange("p a n -> p (a n)").bitcast(F32)
        att_bytes = att[:, :, :].rearrange("p r n -> p (r n)")
        NW = 8
        weights = att_bytes[:, 0:NW * CH // 2].bitcast(BF16).rearrange("p (r n) -> p r n", r=NW)
        weight_bits = att_bytes[:, 0:NW * CH // 2].bitcast(I16).rearrange("p (r n) -> p r n", r=NW)
        squares = att_bytes.rearrange("p (r n) -> p r n", r=3)
        qk_rows = squares[:, 2, :].rearrange("p (t w) -> p t w", t=QT)
        tmp_v = att_bytes[:, 2048:2560].rearrange("p (r t d) -> p r t d", r=2, t=CT)
        h_turned = att_bytes[:, 0:2 * CH].rearrange("p (r n) -> p r n", r=2)

        ps = ctx.enter_context(nc.psum_tensor("ps", [P, 8, CH], F32))
        ps_flat = ps[:, :, :].rearrange("p b n -> p (b n)")
        ps16 = ps_flat.bitcast(F16).rearrange("p (b n) -> p b n", b=8)

        x_loaded = [sem(f"x_loaded{g}") for g in range(2)]
        small_loaded = sem("small_loaded")
        adj_loaded = [[sem(f"adj_loaded{c}_{h}") for h in range(2)] for c in range(C)]
        consts_cast = sem("consts_cast")
        ones_set = sem("ones_set")
        scal_spread = sem("scal_spread")
        scal_copied = sem("scal_copied")
        exps_ready = sem("exps_ready")
        z_params = sem("z_params")
        dve_step = sem("dve_step")
        pool_step = sem("pool_step")
        ln_squares = sem("ln_squares")
        ln_centred = sem("ln_centred")
        h_ready = sem("h_ready")
        h_turned_ps = sem("h_turned_ps")
        h_turned_sb = sem("h_turned_sb")
        lin_ready = sem("lin_ready")
        lin_acted = sem("lin_acted")
        feat_ready = sem("feat_ready")
        f_turned_ps = sem("f_turned_ps")
        f_turned_sb = sem("f_turned_sb")
        qk_ready = sem("qk_ready")
        qk_acted = sem("qk_acted")
        qk_pairs = sem("qk_pairs")
        pairs_turned = sem("pairs_turned")
        pairs_stored = sem("pairs_stored")
        z_ready = sem("z_ready")
        sig_ready = sem("sig_ready")
        att_ready = sem("att_ready")
        att_used = sem("att_used")
        y_copied = [sem(f"y_copied{l}") for l in range(4)]
        node_dve = [sem(f"node_dve{l}") for l in range(3)]
        node_pool = [sem(f"node_pool{l}") for l in range(3)]
        rank_ready = sem("rank_ready")
        weight_act = sem("weight_act")
        weight_dve = sem("weight_dve")
        weight_used = sem("weight_used")
        sum_ready = {l: sem(f"sum_ready{l}") for l in (2, 3)}
        sum_copied = [sem(f"sum_copied{l}") for l in range(4)]
        count_ready = sem("count_ready")
        deg_read = sem("deg_read")
        deg_ready = sem("deg_ready")
        y_ready = [sem(f"y_ready{l}") for l in range(4)]
        h3_turned_ps = sem("h3_turned_ps")
        h3_turned_sb = sem("h3_turned_sb")
        out_ready = sem("out_ready")
        out_stored = sem("out_stored")

        def chunk_tiles(c):
            return slice(c * CT, (c + 1) * CT)

        L0_CHUNKS = list(range(C))[::-1]
        STEPS = T // 2
        L0 = [(c, (k + STEPS // 2) % STEPS) for c in L0_CHUNKS for k in range(STEPS)]
        ROUND = C // 2
        L1 = [(r, b, r * ROUND + q) for r in range(2) for b in range(T)[::-1] for q in range(ROUND)]
        OPEN = 6
        BY_DVE = {0: [], 1: [4, 6], 2: [0, 2, 4, 6]}
        BY_POOL = {0: L0_CHUNKS, 1: [0, 1, 2, 3, 5, 7], 2: [1, 3, 5, 7]}

        def wait_updated(eng, layer, chunks):
            for by, done in ((BY_DVE[layer], node_dve[layer]), (BY_POOL[layer], node_pool[layer])):
                last = max([by.index(c) + 1 for c in chunks if c in by], default=0)
                if last:
                    eng.wait_ge(done, last)

        def chain(eng, counter):
            n = [0]

            def do(ins):
                n[0] += 1
                ins.then_inc(counter, 1)
                eng.wait_ge(counter, n[0])
            return do

        def rsqrt(eng, do, y, v, t, vh):
            do(eng.tensor_scalar(y.bitcast(I32), v.bitcast(I32), -0.5, RSQRT_SEED, ALU.mult, ALU.add))
            do(eng.tensor_scalar(vh, v, -0.5, None, ALU.mult))
            for _ in range(3):
                do(eng.tensor_tensor(t, y, y, ALU.mult))
                do(eng.tensor_tensor(t, t, vh, ALU.mult))
                do(eng.tensor_scalar(t, t, 1.5, None, ALU.add))
                do(eng.tensor_tensor(y, y, t, ALU.mult))

        def row_sum(eng, do, total, v, work):
            if eng is not gpsimd:
                do(eng.tensor_reduce(total, v, AX.X, ALU.add))
                return
            width = D // 2
            do(eng.tensor_tensor(work[:, :, 0:width], v[:, :, 0:width], v[:, :, width:D], ALU.add))
            while width > 2:
                width //= 2
                do(eng.tensor_tensor(work[:, :, 0:width], work[:, :, 0:width], work[:, :, width:2 * width], ALU.add))
            do(eng.tensor_tensor(total, work[:, :, 0], work[:, :, 1], ALU.add))

        def spread(v, n):
            return v.unsqueeze(2).to_broadcast([P, v.shape[1], n])

        def node_update(eng, do, layer, c, y, s, tmp, pairs, done):
            tiles = chunk_tiles(c)
            X, H = x[:, tiles, :], feat[:, tiles, :]
            a, b = tmp[:, 0], tmp[:, 1]
            if layer == 0:
                do(eng.tensor_tensor(a, y, y, ALU.mult))
                do(eng.tensor_scalar(a[:, :, 0], a[:, :, 0], -1.0, None, ALU.mult))
                row_sum(eng, do, s[:, 0], a, a)
                do(eng.tensor_scalar(s[:, 1], s[:, 0], -1.0, 0.0, ALU.mult, ALU.max))
                do(eng.tensor_scalar(s[:, 0], s[:, 0], 0.0, None, ALU.max))
                do(eng.tensor_tensor(s[:, 0], s[:, 0], s[:, 1], ALU.add))
                do(eng.tensor_scalar(s[:, 0], s[:, 0], TINY, None, ALU.max))
                rsqrt(eng, do, s[:, 1], s[:, 0], s[:, 2], s[:, 3])
                do(eng.tensor_tensor(a, y, spread(s[:, 1], D), ALU.mult))
                do(eng.tensor_tensor(X, X, a, ALU.add))
            elif layer == 1:
                do(eng.tensor_tensor(X, X, y, ALU.add))
            else:
                do(eng.tensor_tensor(a, H, y, ALU.mult))
                row_sum(eng, do, s[:, 0], a, a)
                do(eng.tensor_scalar(s[:, 0], s[:, 0], -0.01, 1.0, ALU.mult, ALU.add))
                do(eng.tensor_scalar(b, H, -0.1, None, ALU.mult))
                do(eng.tensor_tensor(b, b, spread(s[:, 0], D), ALU.add))
                do(eng.tensor_tensor(X, X, b, ALU.add))
            row_sum(eng, do, s[:, 0], X, a)
            do(eng.tensor_scalar(s[:, 0], s[:, 0], -1.0 / D, None, ALU.mult))
            do(eng.tensor_tensor(a, X, spread(s[:, 0], D), ALU.add))
            do(eng.tensor_tensor(b, a, a, ALU.mult))
            row_sum(eng, do, s[:, 1], b, b)
            do(eng.tensor_scalar(s[:, 1], s[:, 1], 1.0 / D, EPS, ALU.mult, ALU.add))
            rsqrt(eng, do, s[:, 2], s[:, 1], s[:, 3], s[:, 4])
            do(eng.tensor_scalar(a, a, 0.0, None, ALU.max))
            h = H if layer > 0 else b
            do(eng.tensor_tensor(h, a, spread(s[:, 2], D), ALU.mult))
            hi, lo = pairs[:, tiles, 0:D], pairs[:, tiles, D:2 * D]
            do(eng.tensor_scalar(hi, h, 1.0, None, ALU.mult))
            do(eng.tensor_tensor(a, h, hi, ALU.subtract))
            eng.tensor_scalar(lo, a, LO, None, ALU.mult).then_inc(done, 1)
            eng.wait_ge(done, (BY_POOL if eng is gpsimd else BY_DVE)[layer].index(c) + 1)

        gpsimd = nc.gpsimd
        block = ctx.enter_context(nc.Block())

        @block.sync
        def _(sp):
            xr = x_in.rearrange("(t p) d -> p t d", p=P)
            for g in (1, 0):
                sp.dma_start(x[:, g * GT:(g + 1) * GT, :], xr[:, g * GT:(g + 1) * GT, :]).then_inc(x_loaded[g], 16)
            for dst, src in ((consts, consts_in), (w0, w0_in), (wqk, wqk_in), (scal_row, scalars_in),
                             (rank_f32, rank_in), (c1, w1_in), (bias1, bias1_in), (w3h, w3h_in), (c3, w3n_in)):
                sp.dma_start(dst[:, :], src).then_inc(small_loaded, 16)
            outr = out.rearrange("(t p) d -> p t d", p=P)
            for c in range(C):
                sp.wait_ge(out_ready, c + 1)
                sp.dma_start(outr[:, chunk_tiles(c), :], x[:, chunk_tiles(c), :]).then_inc(out_stored, 16)
            sp.wait_ge(out_stored, 16 * C)

        @block.gpsimd
        def _(pool):
            for c in L0_CHUNKS:
                for h in (1, 0):
                    dst = adj8[:, c, h * HALF:(h + 1) * HALF, :].rearrange("p b n -> p (b n)")
                    src = adj_in[:, c, h * HALF * CH:(h + 1) * HALF * CH]
                    pool.dma_start(dst, src, max_dma_last_dim=2048).then_inc(adj_loaded[c][h], 16)
            assert pool is gpsimd
            do = chain(pool, pool_step)
            pool.wait_ge(pairs_stored, 3 * T // QT)
            for layer, pairs in ((0, pairs_a), (1, pairs_b), (2, pairs_a)):
                for c in BY_POOL[layer]:
                    n = L0_CHUNKS.index(c) if layer == 0 else c
                    pool.wait_ge(y_copied[layer], n + 1)
                    node_update(pool, do, layer, c, ysb[:, n % 4], stp, tmp_p, pairs, node_pool[layer])

        @block.scalar
        def _(act):
            act.wait_ge(scal_spread, 1)
            act.activation(scal[:, :], ps[:, 7, 0:5], ACT.Copy).then_inc(scal_copied, 1)
            act.wait_ge(scal_copied, 1)
            act.activation(exps[:, :], scal[:, 0:3], ACT.Exp).then_inc(exps_ready, 1)
            for g in range(2):
                act.wait_ge(ln_centred, g + 1)
                if g:
                    act.wait_ge(h_ready, 1)
                for q in range(2):
                    tiles = slice((1 - g) * GT + q * QT, (1 - g) * GT + (q + 1) * QT)
                    act.activation(squares[:, 0, q * QT * D:(q + 1) * QT * D].rearrange("p (t d) -> p t d", d=D),
                                   feat[:, tiles, :], ACT.Square).then_inc(ln_squares, 1)

            def turned_to_sb(g, ps_sem, sb_sem):
                act.wait_ge(ps_sem, g + 1)
                act.activation(turned[0:D, g, :], ps_flat[0:D, 0:GT * P], ACT.Copy).then_inc(sb_sem, 1)

            def lorentz_inputs(view, sq, times, ready, n, acted):
                act.wait_ge(ready, n + 1)
                act.activation(times, view[..., 0], ACT.Sigmoid).then_inc(acted, 1)
                act.activation(sq, view, ACT.Square).then_inc(acted, 1)

            turned_to_sb(0, h_turned_ps, h_turned_sb)
            turned_to_sb(1, h_turned_ps, h_turned_sb)
            for g in range(2):
                lin = ps_flat[:, (4 + 2 * g) * CH:(6 + 2 * g) * CH].rearrange("p (t d) -> p t d", d=D)
                lorentz_inputs(lin, squares[:, 1 + g, :].rearrange("p (t d) -> p t d", d=D),
                               st[:, 0, g * GT:(g + 1) * GT], lin_ready, g, lin_acted)
            turned_to_sb(0, f_turned_ps, f_turned_sb)

            def qk_inputs(u):
                if u >= 2:
                    act.wait_ge(qk_pairs, u - 1)
                lin = ps_flat[:, (4 + 2 * (u % 2)) * CH:(6 + 2 * (u % 2)) * CH]
                lorentz_inputs(lin.rearrange("p (t s d) -> p t s d", s=2, d=D),
                               squares[:, u % 2, :].rearrange("p (t s d) -> p t s d", s=2, d=D),
                               st[:, 0, (u % 2) * 2 * QT:(u % 2 + 1) * 2 * QT].rearrange("p (t s) -> p t s", s=2),
                               qk_ready, u, qk_acted)

            qk_inputs(0)
            turned_to_sb(1, f_turned_ps, f_turned_sb)
            for u in range(4):
                if u + 1 < 4:
                    qk_inputs(u + 1)
                tiles = (1 - u // 2) * GT + u % 2 * QT
                cols = slice(tiles * P, (tiles + QT) * P)
                for m, dst in enumerate((keys[:, 0, cols], keys[:, 1, cols], queries[:, cols])):
                    act.wait_ge(pairs_turned, 3 * u + m + 1)
                    act.activation(dst, ps16[:, m, :], ACT.Copy).then_inc(pairs_stored, 1)

            act.wait_ge(z_params, 1)
            for n in range(len(L0) + 3):
                if n < len(L0):
                    act.wait_ge(z_ready, n + 1)
                    z = ps[:, 2 * (n % 3):2 * (n % 3) + 2, :]
                    act.activation(z, z, ACT.Sigmoid, scale=zscale[:, :], bias=zbias[:, :]).then_inc(sig_ready, 1)
                if n >= STEPS and n % STEPS == 2 or n == len(L0) + 2:
                    i = (n - 3) // STEPS
                    act.wait_ge(att_used, (i + 1) * STEPS)
                    if i >= 4:
                        wait_updated(act, 0, [L0_CHUNKS[i - 4]])
                    act.activation(ysb[:, i % 4], ps[:, 6 + i % 2, 0:CT * D].rearrange("p (t d) -> p t d", d=D),
                                   ACT.Copy).then_inc(y_copied[0], 1)

            for r in range(2):
                for n in range(r * len(L1) // 2, (r + 1) * len(L1) // 2):
                    if n % 2 == 0:
                        act.wait_ge(rank_ready, n + 1)
                        if n >= NW:
                            act.wait_ge(weight_used, n - NW + 1)
                        act.activation(weight_bits[:, n % NW, :], ps[:, L1[n][2] % ROUND, :], ACT.Relu)\
                           .then_inc(weight_act, 1)
                for q in range(ROUND):
                    c = r * ROUND + q
                    act.wait_ge(weight_used, (r + 1) * len(L1) // 2 - ROUND + q + 1)
                    act.activation(sums[:, q, :], ps[:, 4 + q, :], ACT.Copy).then_inc(sum_copied[1], 1)
                for q in range(ROUND):
                    c = r * ROUND + q
                    act.wait_ge(y_ready[1], c + 1)
                    if c < 4:
                        wait_updated(act, 0, L0_CHUNKS[4:])
                    else:
                        wait_updated(act, 1, [c - 4])
                    act.activation(ysb[:, c % 4], ps[:, q, 0:CT * D].rearrange("p (t d) -> p t d", d=D), ACT.Copy).then_inc(y_copied[1], 1)

            for c in range(C):
                act.wait_ge(sum_ready[2], c + 1)
                act.activation(sums[:, c % 4, :], ps[:, c % OPEN, :], ACT.Copy).then_inc(sum_copied[2], 1)
                act.wait_ge(y_ready[2], c + 1)
                if c < 4:
                    wait_updated(act, 1, [c + 4])
                else:
                    wait_updated(act, 2, [c - 4])
                act.activation(ysb[:, c % 4], ps[:, 6 + c % 2, 0:CT * D].rearrange("p (t d) -> p t d", d=D),
                               ACT.Copy).then_inc(y_copied[2], 1)

            for c in range(C):
                act.wait_ge(h3_turned_ps, c + 1)
                if c >= 2:
                    act.wait_ge(y_ready[3], c - 1)
                act.activation(h_turned[0:D, c % 2, :], ps[0:D, 6, :], ACT.Copy).then_inc(h3_turned_sb, 1)

        @block.tensor
        def _(pe):
            pe.wait_ge(small_loaded, 16 * 9)
            pe.wait_ge(ones_set, 1)
            pe.matmul(ps[:, 7, 0:5], ones_row[:, :], scal_row[:, :], start=True, stop=True).then_inc(scal_spread, 1)
            pe.wait_ge(scal_copied, 1)

            def turn(g, ready, ps_sem, free_sem, n):
                pe.wait_ge(ready, g + 1)
                if n:
                    pe.wait_ge(free_sem, n)
                for t in range(GT):
                    last = pe.transpose(ps_flat[0:D, t * P:(t + 1) * P], feat[:, (1 - g) * GT + t, :], ident)
                last.then_inc(ps_sem, 1)

            def linear(g):
                pe.wait_ge(h_turned_sb, g + 1)
                for t in range(GT):
                    last = pe.matmul(ps_flat[:, (4 + 2 * g) * CH + t * D:(4 + 2 * g) * CH + (t + 1) * D],
                                     turned[0:D + 1, g, t * P:(t + 1) * P], w0[:, :], start=t % 8 == 0, stop=True,
                                     skip_group_check=True)
                last.then_inc(lin_ready, 1)

            def linear_qk(u):
                pe.wait_ge(f_turned_sb, u // 2 + 1)
                if u < 2:
                    pe.wait_ge(feat_ready, u + 1)
                else:
                    pe.wait_ge(qk_pairs, u - 1)
                for t in range(QT):
                    b = 4 + 2 * (u % 2) + t // 4
                    last = pe.matmul(ps[:, b, (t % 4) * P:(t % 4 + 1) * P],
                                     turned[0:D + 1, u // 2, (u % 2 * QT + t) * P:(u % 2 * QT + t + 1) * P],
                                     wqk[:, :], start=t % 4 == 0, stop=True, skip_group_check=True)
                last.then_inc(qk_ready, 1)

            def turn_pairs(u):
                pe.wait_ge(qk_pairs, u + 1)
                if u == 0:
                    pe.wait_ge(f_turned_sb, 2)
                for m, at in enumerate((D, 0, 3 * D)):
                    if u:
                        pe.wait_ge(pairs_stored, 3 * (u - 1) + m + 1)
                    for t in range(QT):
                        last = pe.transpose(ps16[:, m, t * P:(t + 1) * P], pair_rows[:, t, at:at + P], ident16[:, :])
                    last.then_inc(pairs_turned, 1)

            turn(0, h_ready, h_turned_ps, None, 0)
            pe.wait_ge(ones_set, 3)
            linear(0)
            turn(1, h_ready, h_turned_ps, h_turned_sb, 1)
            linear(1)
            turn(0, feat_ready, f_turned_ps, h_turned_sb, 2)
            linear_qk(0)
            turn(1, feat_ready, f_turned_ps, f_turned_sb, 1)
            linear_qk(1)
            for u in range(4):
                turn_pairs(u)
                if u + 2 < 4:
                    linear_qk(u + 2)

            LAG = 2
            for n in range(len(L0) + LAG):
                if n < len(L0):
                    c, k = L0[n]
                    if n == 0:
                        pe.wait_ge(pairs_stored, 3 * T // QT)
                    if n >= 3:
                        pe.wait_ge(att_ready, n - 2)
                    for h in range(2):
                        z = ps[:, 2 * (n % 3) + h, :]
                        j = slice((2 * k + h) * P, (2 * k + h + 1) * P)
                        q = queries[:, c * CH:(c + 1) * CH]
                        pe.matmul(z, keys[:, 0, j], q, start=True, stop=False)
                        last = pe.matmul(z, keys[:, 1, j], q, start=False, stop=True)
                    last.then_inc(z_ready, 1)
                if n >= LAG:
                    m = n - LAG
                    c, k = L0[m]
                    i, first = m // STEPS, m % STEPS == 0
                    if first and i >= 2:
                        pe.wait_ge(y_copied[0], i - 1)
                    pe.wait_ge(att_ready, m + 1)
                    for h in range(2):
                        for t in range(CT):
                            last = pe.matmul(ps[:, 6 + i % 2, t * D:(t + 1) * D],
                                             att[:, m % 3, h * CH + t * P:h * CH + (t + 1) * P],
                                             feat[:, 2 * k + h, :], start=first and h == 0 and t == 0,
                                             stop=m % STEPS == STEPS - 1 and h == 1, skip_group_check=True)
                    last.then_inc(att_used, 1)

            def combine(layer, c, slot, bank):
                pe.wait_ge(sum_copied[layer], c + 1)
                for t in range(CT):
                    y = ps[:, bank, t * D:(t + 1) * D]
                    w = {1: c1[:, :], 2: c2, 3: c3[:, :]}[layer]
                    last = pe.matmul(y, sums[:, slot, t * P:(t + 1) * P], w, start=t == 0, stop=layer == 2,
                                     skip_group_check=True)
                    if layer == 1:
                        last = pe.matmul(y, ones_row[:, :], bias1[:, :], start=False, stop=True,
                                         skip_group_check=True)
                    if layer == 3:
                        last = pe.matmul(y, h_turned[0:D, c % 2, t * P:(t + 1) * P], w3h[:, :], start=False,
                                         stop=True, skip_group_check=True)
                last.then_inc(y_ready[layer], 1)

            pe.wait_ge(consts_cast, 5)
            HALF1 = len(L1) // 2
            for r in range(2):
                for s in range(HALF1 + LAG):
                    if s < HALF1:
                        n = r * HALF1 + s
                        _, b, c = L1[n]
                        q = c % ROUND
                        if r == 0 and s == 0:
                            pe.wait_ge(att_ready, len(L0))
                        if r == 1 and s < ROUND:
                            pe.wait_ge(y_copied[1], s + 1)
                        pe.matmul(ps[:, q, :], rank_w[:, :], adj8[:, c, b, :], start=b == T - 1, stop=True,
                                  skip_group_check=True).then_inc(rank_ready, 1)
                    if s >= LAG:
                        n = r * HALF1 + s - LAG
                        _, b, c = L1[n]
                        q = c % ROUND
                        if n % 2 == 0:
                            pe.wait_ge(weight_act, n // 2 + 1)
                        else:
                            pe.wait_ge(weight_dve, n // 2 + 1)
                        last = pe.matmul(ps[:, q, :], carry_w[:, :], adj8[:, c, b, :], start=False, stop=True,
                                         skip_group_check=True)
                        if b == 0:
                            last.then_inc(count_ready, 1)
                        if r == 0 and b % CT == CT - 1:
                            wait_updated(pe, 0, [b // CT])
                        if r == 0 and b == T - 1:
                            pe.wait_ge(y_copied[0], C)
                        if r == 1 and b == T - 1:
                            pe.wait_ge(sum_copied[1], ROUND)
                        last = pe.matmul(ps[:, 4 + q, :], pairs_a[:, b, :], weights[:, n % NW, :], start=b == T - 1,
                                         stop=b == 0)
                        last.then_inc(weight_used, 1)
                for q in range(ROUND):
                    if q == 0:
                        pe.wait_ge(deg_read, r * ROUND + ROUND)
                    combine(1, r * ROUND + q, q, q)

            def aggregate(layer, pairs, c, blocks, first, final):
                for b in blocks:
                    last = pe.matmul(ps[:, c % OPEN, :], pairs[:, b, :], adj8[:, c, b, :],
                                     start=first and b == blocks[0], stop=final and b == blocks[-1])
                if final:
                    last.then_inc(sum_ready[layer], 1)

            def chunk_blocks(a, b):
                return list(range(a * CT, b * CT))

            for layer, pairs in ((2, pairs_b), (3, pairs_a)):
                segments = [(0, 4), (4, 6), (6, 8)]
                for a, b in segments[:-1]:
                    wait_updated(pe, layer - 1, range(a, b))
                    for c in range(OPEN):
                        if a == 0 and layer == 2:
                            pe.wait_ge(y_copied[1], C)
                        if a == 0 and layer == 3:
                            pe.wait_ge(sum_copied[2], c + 1 + (OPEN if c < C - OPEN else 0))
                        aggregate(layer, pairs, c, chunk_blocks(a, b), a == 0, False)
                a, b = segments[-1]
                wait_updated(pe, layer - 1, range(a, b))
                for c in range(C + 1):
                    if c < C:
                        if c < OPEN:
                            aggregate(layer, pairs, c, chunk_blocks(a, b), False, True)
                        else:
                            pe.wait_ge(sum_copied[layer], c - OPEN + 1)
                            aggregate(layer, pairs, c, chunk_blocks(0, b), True, True)
                    if c >= 1:
                        m = c - 1
                        if layer == 2:
                            if m >= 2:
                                pe.wait_ge(y_copied[2], m - 1)
                            combine(2, m, m % 4, 6 + m % 2)
                        else:
                            if m == 0:
                                pe.wait_ge(y_copied[2], C)
                            for t in range(CT):
                                last = pe.transpose(ps[0:D, 6, t * P:(t + 1) * P], feat[:, m * CT + t, :], ident)
                            last.then_inc(h3_turned_ps, 1)
                            pe.wait_ge(h3_turned_sb, m + 1)
                            if m:
                                pe.wait_ge(out_ready, m)
                            combine(3, m, m % 4, 7)

        @block.vector
        def _(dve):
            do = chain(dve, dve_step)
            dve.memset(ones_row[:, :], 1.0).then_inc(ones_set, 1)
            for r in range(2):
                dve.memset(turned[D:D + 1, r, :], 1.0).then_inc(ones_set, 1)

            for g in range(2):
                tiles = slice((1 - g) * GT, (2 - g) * GT)
                X, H = x[:, tiles, :], feat[:, tiles, :]
                dve.wait_ge(x_loaded[1 - g], 16)
                do(dve.tensor_reduce(st[:, 1, 0:GT], X, AX.X, ALU.add))
                dve.scalar_tensor_tensor(H, spread(st[:, 1, 0:GT], D), -1.0 / D, X, ALU.mult, ALU.add)\
                   .then_inc(ln_centred, 1)
                dve.wait_ge(ln_squares, 2 * g + 2)
                sq = squares[:, 0, :].rearrange("p (t d) -> p t d", d=D)
                do(dve.tensor_reduce(st[:, 2, 0:GT], sq, AX.X, ALU.add))
                do(dve.tensor_scalar(st[:, 2, 0:GT], st[:, 2, 0:GT], 1.0 / D, EPS, ALU.mult, ALU.add))
                rsqrt(dve, do, st[:, 3, 0:GT], st[:, 2, 0:GT], st[:, 4, 0:GT], st[:, 5, 0:GT])
                dve.scalar_tensor_tensor(H, H, 0.0, spread(st[:, 3, 0:GT], D), ALU.max, ALU.mult)\
                   .then_inc(h_ready, 1)

            dve.wait_ge(exps_ready, 1)
            do(dve.reciprocal(zscale[:, :], scal[:, 4:5]))
            do(dve.tensor_scalar(zscale[:, :], zscale[:, :], 2.0, None, ALU.mult))
            dve.tensor_tensor(zbias[:, :], zscale[:, :], scal[:, 3:4], ALU.add).then_inc(z_params, 1)
            dve.wait_ge(small_loaded, 16 * 9)
            dve.tensor_copy(ident16[:, :], ident).then_inc(consts_cast, 1)
            dve.tensor_copy(rank_w[:, :], rank_f32[:, 0:P]).then_inc(consts_cast, 1)
            dve.tensor_copy(carry_w[:, :], rank_f32[:, P:2 * P]).then_inc(consts_cast, 1)
            dve.tensor_scalar(c1[:, :], c1[:, :], hilo1, None, ALU.mult).then_inc(consts_cast, 1)
            dve.tensor_scalar(c3[:, :], c3[:, :], hilo3, None, ALU.mult).then_inc(consts_cast, 1)

            def lorentz_factor(times, sums_, a, f, s1, s2):
                do(dve.tensor_scalar(sums_, sums_, TINY, None, ALU.max))
                do(dve.reciprocal(sums_, sums_))
                do(dve.tensor_tensor(a, times, times, ALU.mult))
                do(dve.scalar_tensor_tensor(a, a, 1.0, sums_, ALU.subtract, ALU.mult))
                rsqrt(dve, do, f, a, s1, s2)
                do(dve.tensor_tensor(f, f, a, ALU.mult))

            for g in range(2):
                lin = ps_flat[:, (4 + 2 * g) * CH:(6 + 2 * g) * CH].rearrange("p (t d) -> p t d", d=D)
                sq = squares[:, 1 + g, :].rearrange("p (t d) -> p t d", d=D)
                S = [st[:, k, g * GT:(g + 1) * GT] for k in range(6)]
                dve.wait_ge(lin_acted, 2 * g + 2)
                do(dve.tensor_reduce(S[1], sq[:, :, 1:D], AX.X, ALU.add))
                do(dve.tensor_scalar(S[0], S[0], exps[:, 0:1], 1.1, ALU.mult, ALU.add))
                lorentz_factor(S[0], S[1], S[2], S[3], S[4], S[5])
                F = feat[:, (1 - g) * GT:(2 - g) * GT, :]
                dve.wait_ge(h_turned_ps, g + 1)
                do(dve.tensor_tensor(F, lin, spread(S[3], D), ALU.mult))
                dve.tensor_copy(F[:, :, 0], S[0]).then_inc(feat_ready, 1)

            for u in range(4):
                lin = ps_flat[:, (4 + 2 * (u % 2)) * CH:(6 + 2 * (u % 2)) * CH].rearrange("p (t s d) -> p t s d", s=2, d=D)
                sq = squares[:, u % 2, :].rearrange("p (t s d) -> p t s d", s=2, d=D)
                S = [st[:, k, (u % 2) * 2 * QT:(u % 2 + 1) * 2 * QT] for k in range(6)]
                S2 = [v.rearrange("p (t s) -> p t s", s=2) for v in S]
                dve.wait_ge(qk_acted, 2 * u + 2)
                do(dve.tensor_reduce(S2[1], sq[:, :, :, 1:D], AX.X, ALU.add))
                do(dve.tensor_tensor(S2[0], S2[0], exps[:, 1:3].unsqueeze(1).to_broadcast([P, QT, 2]), ALU.mult))
                do(dve.tensor_scalar(S[0], S[0], 1.1, None, ALU.add))
                lorentz_factor(S[0], S[1], S[2], S[3], S[4], S[5])
                rows = qk_rows.rearrange("p t (s d) -> p t s d", s=2)
                do(dve.tensor_tensor(rows, lin, S2[3].unsqueeze(3).to_broadcast([P, QT, 2, D]), ALU.mult))
                do(dve.tensor_scalar(rows[:, :, 0, 0], S2[0][:, :, 0], -1.0, None, ALU.mult))
                do(dve.tensor_copy(rows[:, :, 1, 0], S2[0][:, :, 1]))
                if u:
                    dve.wait_ge(pairs_turned, 3 * u)
                q, k = rows[:, :, 0, :], rows[:, :, 1, :]
                klo, khi, klo2, qhi, qlo = (pair_rows[:, :, m * D:(m + 1) * D] for m in range(5))
                do(dve.tensor_copy(khi, k))
                do(dve.tensor_copy(qhi, q))
                do(dve.tensor_tensor(klo, k, khi, ALU.subtract))
                do(dve.tensor_tensor(qlo, q, qhi, ALU.subtract))
                dve.tensor_copy(klo2, klo).then_inc(qk_pairs, 1)

            for n, (c, k) in enumerate(L0):
                dve.wait_ge(sig_ready, n + 1)
                if n < 2 * STEPS or k % (STEPS // 2) == 0:
                    dve.wait_ge(adj_loaded[c][1 if 2 * k >= HALF else 0], 16)
                if n >= 3:
                    dve.wait_ge(att_used, n - 2)
                dve.tensor_tensor(att[:, n % 3, :].rearrange("p (h i) -> p h i", h=2),
                                  ps[:, 2 * (n % 3):2 * (n % 3) + 2, :],
                                  adj8[:, c, 2 * k:2 * k + 2, :], ALU.mult).then_inc(att_ready, 1)

            for r in range(2):
                for n in range(r * len(L1) // 2, (r + 1) * len(L1) // 2):
                    if n % 2 == 1:
                        dve.wait_ge(rank_ready, n + 1)
                        if n >= NW:
                            dve.wait_ge(weight_used, n - NW + 1)
                        dve.tensor_scalar(weight_bits[:, n % NW, :], ps[:, L1[n][2] % ROUND, :], 0.0, None, ALU.max)\
                           .then_inc(weight_dve, 1)
                for q in range(ROUND):
                    c = r * ROUND + q
                    dve.wait_ge(count_ready, c + 1)
                    dve.tensor_scalar(rdeg[:, c * CH:(c + 1) * CH], ps[:, q, :], -1.0 / P, 1.0, ALU.mult, ALU.max)\
                       .then_inc(deg_read, 1)
                dve.wait_ge(deg_read, (r + 1) * ROUND)
                for q in range(ROUND):
                    c = r * ROUND + q
                    dve.reciprocal(rdeg[:, c * CH:(c + 1) * CH], rdeg[:, c * CH:(c + 1) * CH]).then_inc(deg_ready, 1)
            for layer, pairs in ((1, pairs_b), (2, pairs_a)):
                for c in BY_DVE[layer]:
                    dve.wait_ge(y_copied[layer], c + 1)
                    node_update(dve, do, layer, c, ysb[:, c % 4], st[:, :, 0:CT], tmp_v, pairs, node_dve[layer])

            dve.wait_ge(deg_ready, C)
            for c in range(C + 1):
                if c < C:
                    dve.wait_ge(sum_ready[3], c + 1)
                    if c == 0:
                        dve.wait_ge(y_ready[2], C)
                    if c >= 4:
                        dve.wait_ge(y_ready[3], c - 3)
                    dve.tensor_tensor(sums[:, c % 4, :], ps[:, c % OPEN, :], rdeg[:, c * CH:(c + 1) * CH], ALU.mult)\
                       .then_inc(sum_copied[3], 1)
                if c >= 1:
                    m = c - 1
                    dve.wait_ge(y_ready[3], m + 1)
                    X = x[:, chunk_tiles(m), :]
                    dve.scalar_tensor_tensor(X, ps[:, 7, 0:CT * D].rearrange("p (t d) -> p t d", d=D), 0.0, X,
                                             ALU.max, ALU.add).then_inc(out_ready, 1)


def kernel(**inputs):
    import numpy as np
    import concourse.bacc as bacc
    from concourse.bass_utils import run_bass_kernel_spmd

    a = {k: np.asarray(v) for k, v in inputs.items()}
    N, D = a["x"].shape
    T, C = N // 128, 8

    consts = np.zeros((128, NC_), np.float32)
    consts[:, 0:128] = np.eye(128)
    consts[:, 128:192] = np.concatenate([np.eye(D), np.eye(D) * 2.0 ** -11])
    j = np.arange(128)
    rank = 128.0 * (100.0 * np.eye(128) - (j[:, None] > j[None, :]))
    consts[:, 192] = np.where(j < D, 2.0 ** 27, 2.0 ** 16)
    consts[:, 193] = np.where(j < D, 1.0, 2.0 ** -11)

    W3 = a["L3_gnn_W"]
    arrays = {
        "x_in": np.ascontiguousarray(a["x"]),
        "adj_in": np.ascontiguousarray(
            a["adj"].T.reshape(T, 128, C, N // C).transpose(1, 2, 0, 3)).reshape(128, C, T * (N // C)),
        "w0_in": np.concatenate([a["L0_gnn_W"].T, a["L0_gnn_b"][None]]),
        "wqk_in": np.concatenate([
            np.concatenate([a["L0_gnn_Wq"].T, a["L0_gnn_bq"][None]]),
            np.concatenate([a["L0_gnn_Wk"].T, a["L0_gnn_bk"][None]])], axis=1),
        "scalars_in": np.stack([a[k] for k in (
            "L0_gnn_scale", "L0_gnn_scale_q", "L0_gnn_scale_k", "L0_gnn_att_bias", "L0_gnn_att_scale")])[None],
        "w1_in": np.concatenate([a["L1_gnn_weight"]] * 2),
        "bias1_in": a["L1_gnn_bias"][None],
        "w3h_in": np.ascontiguousarray(W3[:, :D].T),
        "w3n_in": np.concatenate([W3[:, D:].T] * 2),
        "consts_in": consts,
        "rank_in": np.concatenate([rank, -128.0 - rank], axis=1).astype(np.float32),
    }
    nc = bacc.Bacc("TRN2", target_bir_lowering=False, num_devices=1)
    args = [nc.dram_tensor(k, v.shape, mybir.dt.from_np(v.dtype), kind="ExternalInput").ap()
            for k, v in arrays.items()]
    out = nc.dram_tensor("out", (N, D), F32, kind="ExternalOutput").ap()
    gnn_program(nc, *args, out)
    r = run_bass_kernel_spmd(nc, [arrays], core_ids=[0])
    return r.results[0]["out"]
```

```python
from contextlib import ExitStack

import concourse.bass as bass
from concourse import mybir

F32 = mybir.dt.float32
F16 = mybir.dt.float16
BF16 = mybir.dt.bfloat16
F8 = mybir.dt.float8e4
I32 = mybir.dt.int32
I16 = mybir.dt.int16
ALU = mybir.AluOpType
ACT = mybir.ActivationFunctionType
AX = mybir.AxisListType

P = 128
LO = 2.0 ** 11
CUT = 100
BIAS = 127
EPS = 1e-5
TINY = 1e-8
FLT_MAX = 3.4028235e38
RSQRT_SEED = float(0x5F3759DF)
NC_ = P + 2 * 64 + 2


def gnn_program(nc, x_in, adj_in, w0_in, wqk_in, scalars_in, w1_in, bias1_in, w3h_in, w3n_in, consts_in, rank_in, out):
    N, D = x_in.shape
    T = N // P
    CH = 512
    CT = CH // P
    C = N // CH
    HALF = T // 2
    assert D == 64 and T == 32 and C == 8

    ctx = ExitStack()
    with ctx:
        def sb(name, shape, dt):
            return ctx.enter_context(nc.sbuf_tensor(name, shape, dt))

        def sem(name):
            return ctx.enter_context(nc.semaphore(name))

        adj8 = sb("adj8", [P, C, T, CH], F8)
        x = sb("x", [P, T, D], F32)
        feat = sb("feat", [P, T, D], F32)
        keys = sb("keys", [P, 2, N], F16)
        queries = sb("queries", [P, N], F16)
        att = sb("att", [P, 3, 2 * CH], F32)
        scratch = sb("scratch", [P, 5632], F32)
        consts = sb("consts", [P, NC_], F32)
        w0 = sb("w0", [D + 1, D], F32)
        wqk = sb("wqk", [D + 1, 2 * D], F32)
        c1 = sb("c1", [P, D], F32)
        c3 = sb("c3", [P, D], F32)
        w3h = sb("w3h", [D, D], F32)
        bias1 = sb("bias1", [1, D], F32)
        scal_row = sb("scal_row", [1, 5], F32)
        ones_row = sb("ones_row", [1, P], F32)
        scal = sb("scal", [P, 5], F32)
        exps = sb("exps", [P, 3], F32)
        zscale = sb("zscale", [P, 1], F32)
        zbias = sb("zbias", [P, 1], F32)
        warm = sb("warm", [P, 1], F32)
        ident16 = sb("ident16", [P, P], F16)
        rank_w = sb("rank_w", [P, P], BF16)
        carry_w = sb("carry_w", [P, P], BF16)
        st = sb("st", [P, 6, HALF], F32)
        stlq = sb("stlq", [P, 6 * 2 * 16], F32)
        stp = sb("stp", [P, 6, CT], F32)
        ident = consts[:, 0:P]
        c2 = consts[:, P:P + D]
        both = consts[:, P + D:P + 2 * D]
        hilo1, hilo3 = consts[:, NC_ - 2:NC_ - 1], consts[:, NC_ - 1:NC_]

        GT = HALF
        QT = 8
        turned = scratch[:, 0:4096].rearrange("p (r n) -> p r n", r=2)
        pair_rows = scratch[:, 4096:5376].bitcast(F16).rearrange("p (t w) -> p t w", t=QT)
        rank_f32 = scratch[:, 4096:4352]
        stl = scratch[:, 5376:5568].rearrange("p (k t) -> p k t", k=6)
        stq = stlq[:, :].rearrange("p (k r t) -> p k r t", k=6, r=2)
        pairs_a = scratch[:, 0:2048].bitcast(F16).rearrange("p (t w) -> p t w", t=T)
        sums = scratch[:, 2048:4096].rearrange("p (r n) -> p r n", r=4)
        ysb = scratch[:, 4096:5120].rearrange("p (r t d) -> p r t d", r=4, t=CT)
        tmp_p = scratch[:, 5120:5632].rearrange("p (r t d) -> p r t d", r=2, t=CT)
        pairs_b = queries[:, :].rearrange("p (t w) -> p t w", t=T)
        rdeg = keys[:, :, :].rearrange("p a n -> p (a n)").bitcast(F32)
        att_bytes = att[:, :, :].rearrange("p r n -> p (r n)")
        NW = 8
        weights = att_bytes[:, 0:NW * CH // 2].bitcast(BF16).rearrange("p (r n) -> p r n", r=NW)
        weight_bits = att_bytes[:, 0:NW * CH // 2].bitcast(I16).rearrange("p (r n) -> p r n", r=NW)
        squares = att_bytes.rearrange("p (r n) -> p r n", r=3)
        qk_rows = squares[:, 2, :].rearrange("p (t w) -> p t w", t=QT)
        tmp_v = att_bytes[:, 2048:2560].rearrange("p (r t d) -> p r t d", r=2, t=CT)
        h_turned = att_bytes[:, 0:2 * CH].rearrange("p (r n) -> p r n", r=2)

        ps = ctx.enter_context(nc.psum_tensor("ps", [P, 8, CH], F32))
        ps_flat = ps[:, :, :].rearrange("p b n -> p (b n)")
        ps16 = ps_flat.bitcast(F16).rearrange("p (b n) -> p b n", b=8)

        x_loaded = [sem(f"x_loaded{g}") for g in range(2)]
        small_loaded = sem("small_loaded")
        scal_loaded = sem("scal_loaded")
        consts_loaded = sem("consts_loaded")
        warmed = sem("warmed")
        adj_loaded = [[sem(f"adj_loaded{c}_{h}") for h in range(2)] for c in range(C)]
        consts_cast = sem("consts_cast")
        ones_set = sem("ones_set")
        scal_spread = sem("scal_spread")
        scal_copied = sem("scal_copied")
        exps_ready = sem("exps_ready")
        z_params = sem("z_params")
        dve_step = sem("dve_step")
        pool_step = sem("pool_step")
        ln_squares = sem("ln_squares")
        lin_summed = sem("lin_summed")
        lin_factor = sem("lin_factor")
        qk_summed = sem("qk_summed")
        qk_factor = sem("qk_factor")
        qk_rows_ready = sem("qk_rows_ready")
        high_ready = sem("high_ready")
        ln_centred = sem("ln_centred")
        h_ready = sem("h_ready")
        h_turned_ps = sem("h_turned_ps")
        h_turned_sb = sem("h_turned_sb")
        lin_ready = sem("lin_ready")
        lin_acted = sem("lin_acted")
        feat_ready = sem("feat_ready")
        f_turned_ps = sem("f_turned_ps")
        f_turned_sb = sem("f_turned_sb")
        qk_ready = sem("qk_ready")
        qk_acted = sem("qk_acted")
        qk_pairs = sem("qk_pairs")
        pairs_turned = sem("pairs_turned")
        pairs_stored = sem("pairs_stored")
        z_ready = sem("z_ready")
        sig_ready = sem("sig_ready")
        att_ready = sem("att_ready")
        att_used = sem("att_used")
        y_copied = [sem(f"y_copied{l}") for l in range(4)]
        node_dve = [sem(f"node_dve{l}") for l in range(3)]
        node_pool = [sem(f"node_pool{l}") for l in range(3)]
        rank_ready = sem("rank_ready")
        weight_act = sem("weight_act")
        weight_dve = sem("weight_dve")
        weight_used = sem("weight_used")
        sum_ready = {l: sem(f"sum_ready{l}") for l in (2, 3)}
        sum_copied = [sem(f"sum_copied{l}") for l in range(4)]
        count_ready = sem("count_ready")
        deg_read = sem("deg_read")
        deg_ready = sem("deg_ready")
        y_ready = [sem(f"y_ready{l}") for l in range(4)]
        h3_turned_ps = sem("h3_turned_ps")
        h3_turned_sb = sem("h3_turned_sb")
        out_ready = sem("out_ready")
        out_stored = sem("out_stored")

        def chunk_tiles(c):
            return slice(c * CT, (c + 1) * CT)

        L0_CHUNKS = list(range(C))[::-1]
        STEPS = T // 2
        L0 = [(c, (k + STEPS // 2) % STEPS) for c in L0_CHUNKS for k in range(STEPS)]
        ROUND = C // 2
        L1 = [(r, b, r * ROUND + q) for r in range(2) for b in range(T)[::-1] for q in range(ROUND)]
        OPEN = 6
        BY_DVE = {0: [], 1: [4, 5, 6], 2: [0, 1, 3, 4, 6, 7]}
        BY_POOL = {0: L0_CHUNKS, 1: [0, 1, 2, 3, 7], 2: [2, 5]}

        def wait_updated(eng, layer, chunks):
            for by, done in ((BY_DVE[layer], node_dve[layer]), (BY_POOL[layer], node_pool[layer])):
                last = max([by.index(c) + 1 for c in chunks if c in by], default=0)
                if last:
                    eng.wait_ge(done, last)

        def chain(eng, counter):
            n = [0]

            def do(ins):
                n[0] += 1
                ins.then_inc(counter, 1)
                eng.wait_ge(counter, n[0])
            return do

        def rsqrt(eng, do, y, v, t, vh):
            do(eng.tensor_scalar(y.bitcast(I32), v.bitcast(I32), -0.5, RSQRT_SEED, ALU.mult, ALU.add))
            do(eng.tensor_scalar(vh, v, -0.5, 1.0, ALU.mult, ALU.mult))
            for _ in range(3):
                do(eng.tensor_tensor(t, y, y, ALU.mult))
                do(eng.tensor_tensor(t, t, vh, ALU.mult))
                if eng is gpsimd:
                    do(eng.tensor_scalar(t, t, 1.0, 1.5, ALU.mult, ALU.add))
                    do(eng.tensor_tensor(y, y, t, ALU.mult))
                else:
                    do(eng.scalar_tensor_tensor(y, t, 1.5, y, ALU.add, ALU.mult))

        def row_sum(eng, do, total, v, work):
            if eng is not gpsimd:
                do(eng.tensor_reduce(total, v, AX.X, ALU.add))
                return
            width = D // 2
            do(eng.tensor_tensor(work[:, :, 0:width], v[:, :, 0:width], v[:, :, width:D], ALU.add))
            while width > 2:
                width //= 2
                do(eng.tensor_tensor(work[:, :, 0:width], work[:, :, 0:width], work[:, :, width:2 * width], ALU.add))
            do(eng.tensor_tensor(total, work[:, :, 0], work[:, :, 1], ALU.add))

        def spread(v, n):
            return v.unsqueeze(2).to_broadcast([P, v.shape[1], n])

        def node_update(eng, do, layer, c, y, s, tmp, pairs, done):
            on_dve = eng is not gpsimd
            tiles = chunk_tiles(c)
            X, H = x[:, tiles, :], feat[:, tiles, :]
            a, b = tmp[:, 0], tmp[:, 1]
            if layer == 0:
                do(eng.tensor_tensor(a, y, y, ALU.mult))
                do(eng.tensor_scalar(a[:, :, 0], a[:, :, 0], -1.0, 1.0, ALU.mult, ALU.mult))
                row_sum(eng, do, s[:, 0], a, a)
                do(eng.tensor_scalar(s[:, 1], s[:, 0], -1.0, 0.0, ALU.mult, ALU.max))
                do(eng.tensor_scalar(s[:, 0], s[:, 0], FLT_MAX, 0.0, ALU.min, ALU.max))
                do(eng.tensor_tensor(s[:, 0], s[:, 0], s[:, 1], ALU.add))
                do(eng.tensor_scalar(s[:, 0], s[:, 0], FLT_MAX, TINY, ALU.min, ALU.max))
                rsqrt(eng, do, s[:, 1], s[:, 0], s[:, 2], s[:, 3])
                do(eng.tensor_tensor(a, y, spread(s[:, 1], D), ALU.mult))
                do(eng.tensor_tensor(X, X, a, ALU.add))
            elif layer == 1:
                do(eng.tensor_tensor(X, X, y, ALU.add))
            else:
                do(eng.tensor_tensor(a, H, y, ALU.mult))
                row_sum(eng, do, s[:, 0], a, a)
                do(eng.tensor_scalar(s[:, 0], s[:, 0], -0.01, 1.0, ALU.mult, ALU.add))
                if on_dve:
                    do(eng.scalar_tensor_tensor(X, H, -0.1, X, ALU.mult, ALU.add))
                    do(eng.tensor_tensor(X, X, spread(s[:, 0], D), ALU.add))
                else:
                    do(eng.tensor_scalar(b, H, -0.1, 1.0, ALU.mult, ALU.mult))
                    do(eng.tensor_tensor(b, b, spread(s[:, 0], D), ALU.add))
                    do(eng.tensor_tensor(X, X, b, ALU.add))
            row_sum(eng, do, s[:, 0], X, a)
            if on_dve:
                do(eng.scalar_tensor_tensor(a, spread(s[:, 0], D), -1.0 / D, X, ALU.mult, ALU.add))
            else:
                do(eng.tensor_scalar(s[:, 0], s[:, 0], -1.0 / D, 1.0, ALU.mult, ALU.mult))
                do(eng.tensor_tensor(a, X, spread(s[:, 0], D), ALU.add))
            do(eng.tensor_tensor(b, a, a, ALU.mult))
            row_sum(eng, do, s[:, 1], b, b)
            do(eng.tensor_scalar(s[:, 1], s[:, 1], 1.0 / D, EPS, ALU.mult, ALU.add))
            rsqrt(eng, do, s[:, 2], s[:, 1], s[:, 3], s[:, 4])
            h = H if layer > 0 else b
            if on_dve:
                do(eng.scalar_tensor_tensor(h, a, 0.0, spread(s[:, 2], D), ALU.max, ALU.mult))
            else:
                do(eng.tensor_scalar(a, a, FLT_MAX, 0.0, ALU.min, ALU.max))
                do(eng.tensor_tensor(h, a, spread(s[:, 2], D), ALU.mult))
            hi, lo = pairs[:, tiles, 0:D], pairs[:, tiles, D:2 * D]
            do(eng.tensor_scalar(hi, h, 1.0, 1.0, ALU.mult, ALU.mult))
            do(eng.tensor_tensor(a, h, hi, ALU.subtract))
            eng.tensor_scalar(lo, a, LO, 1.0, ALU.mult, ALU.mult).then_inc(done, 1)
            eng.wait_ge(done, (BY_DVE if on_dve else BY_POOL)[layer].index(c) + 1)

        gpsimd = nc.gpsimd
        block = ctx.enter_context(nc.Block())

        @block.sync
        def _(sp):
            xr = x_in.rearrange("(t p) d -> p t d", p=P)
            for g in (1, 0):
                sp.dma_start(x[:, g * GT:(g + 1) * GT, :], xr[:, g * GT:(g + 1) * GT, :]).then_inc(x_loaded[g], 16)
            for dst, src in ((w0, w0_in), (wqk, wqk_in), (rank_f32, rank_in), (c1, w1_in), (bias1, bias1_in),
                             (w3h, w3h_in), (c3, w3n_in)):
                sp.dma_start(dst[:, :], src).then_inc(small_loaded, 16)
            outr = out.rearrange("(t p) d -> p t d", p=P)
            for c in range(C):
                sp.wait_ge(out_ready, c + 1)
                sp.dma_start(outr[:, chunk_tiles(c), :], x[:, chunk_tiles(c), :]).then_inc(out_stored, 16)
            sp.wait_ge(out_stored, 16 * C)

        @block.gpsimd
        def _(pool):
            for c in L0_CHUNKS:
                for h in (1, 0):
                    dst = adj8[:, c, h * HALF:(h + 1) * HALF, :].rearrange("p b n -> p (b n)")
                    src = adj_in[:, c, h * HALF * CH:(h + 1) * HALF * CH]
                    pool.dma_start(dst, src, max_dma_last_dim=2048).then_inc(adj_loaded[c][h], 16)
            assert pool is gpsimd
            do = chain(pool, pool_step)

            def lorentz_factor(S, scale_times):
                scale_times()
                do(pool.tensor_tensor(S[2], S[0], S[0], ALU.mult))
                do(pool.tensor_scalar(S[2], S[2], 1.0, -1.0, ALU.mult, ALU.add))
                do(pool.tensor_scalar(S[1], S[1], FLT_MAX, TINY, ALU.min, ALU.max))
                do(pool.tensor_tensor(S[1], S[1], S[2], ALU.mult))
                rsqrt(pool, do, S[3], S[1], S[4], S[5])

            pool.wait_ge(exps_ready, 1)
            for g in range(2):
                S = [stl[:, k, g * GT:(g + 1) * GT] for k in range(6)]
                pool.wait_ge(lin_summed, g + 1)
                lorentz_factor(S, lambda: do(pool.tensor_scalar(S[0], S[0], exps[:, 0:1], 1.1, ALU.mult, ALU.add)))
                pool.tensor_tensor(S[3], S[3], S[2], ALU.mult).then_inc(lin_factor, 1)
            for u in range(4):
                S = [stq[:, k, u % 2, :] for k in range(6)]

                def scale_times():
                    both_times = S[0].rearrange("p (t s) -> p t s", s=2)
                    do(pool.tensor_tensor(both_times, both_times,
                                          exps[:, 1:3].unsqueeze(1).to_broadcast([P, QT, 2]), ALU.mult))
                    do(pool.tensor_scalar(S[0], S[0], 1.0, 1.1, ALU.mult, ALU.add))

                pool.wait_ge(qk_summed, u + 1)
                lorentz_factor(S, scale_times)
                pool.tensor_tensor(S[3], S[3], S[2], ALU.mult).then_inc(qk_factor, 1)

            pool.wait_ge(pairs_stored, 3 * T // QT)
            for layer, pairs in ((0, pairs_a), (1, pairs_b), (2, pairs_a)):
                for c in BY_POOL[layer]:
                    n = L0_CHUNKS.index(c) if layer == 0 else c
                    pool.wait_ge(y_copied[layer], n + 1)
                    node_update(pool, do, layer, c, ysb[:, n % 4], stp, tmp_p, pairs, node_pool[layer])

        @block.scalar
        def _(act):
            act.dma_start(scal_row[:, :], scalars_in).then_inc(scal_loaded, 16)
            act.dma_start(consts[:, :], consts_in).then_inc(consts_loaded, 16)
            act.wait_ge(scal_spread, 1)
            act.activation(scal[:, :], ps[:, 7, 0:5], ACT.Copy).then_inc(scal_copied, 1)
            act.wait_ge(scal_copied, 1)
            act.activation(exps[:, :], scal[:, 0:3], ACT.Exp).then_inc(exps_ready, 1)
            act.wait_ge(exps_ready, 1)
            act.activation(warm[:, :], scal[:, 0:1], ACT.Sigmoid).then_inc(warmed, 1)
            for g in range(2):
                act.wait_ge(ln_centred, g + 1)
                if g:
                    act.wait_ge(h_ready, 1)
                for q in range(2):
                    tiles = slice((1 - g) * GT + q * QT, (1 - g) * GT + (q + 1) * QT)
                    act.activation(squares[:, 0, q * QT * D:(q + 1) * QT * D].rearrange("p (t d) -> p t d", d=D),
                                   feat[:, tiles, :], ACT.Square).then_inc(ln_squares, 1)

            def turned_to_sb(u, ps_sem, sb_sem):
                act.wait_ge(ps_sem, u + 1)
                act.activation(turned[0:D, u // 2, (u % 2) * QT * P:(u % 2 + 1) * QT * P],
                               ps_flat[0:D, (u % 2) * QT * P:(u % 2 + 1) * QT * P], ACT.Copy).then_inc(sb_sem, 1)

            def lorentz_inputs(view, sq, times, ready, n, acted):
                act.wait_ge(ready, n + 1)
                act.activation(times, view[..., 0], ACT.Sigmoid).then_inc(acted, 1)
                act.activation(sq, view, ACT.Square).then_inc(acted, 1)

            def feat_inputs(g):
                lin = ps_flat[:, (4 + 2 * g) * CH:(6 + 2 * g) * CH].rearrange("p (t d) -> p t d", d=D)
                lorentz_inputs(lin, squares[:, 1 + g, :].rearrange("p (t d) -> p t d", d=D),
                               stl[:, 0, g * GT:(g + 1) * GT], lin_ready, 2 * g + 1, lin_acted)

            def qk_inputs(u):
                if u >= 2:
                    act.wait_ge(qk_pairs, u - 1)
                lin = ps_flat[:, (4 + 2 * (u % 2)) * CH:(6 + 2 * (u % 2)) * CH]
                lorentz_inputs(lin.rearrange("p (t s d) -> p t s d", s=2, d=D),
                               squares[:, u % 2, :].rearrange("p (t s d) -> p t s d", s=2, d=D),
                               stq[:, 0, u % 2, :].rearrange("p (t s) -> p t s", s=2),
                               qk_ready, u, qk_acted)

            def high_halves(u):
                act.wait_ge(qk_rows_ready, u + 1)
                if u:
                    act.wait_ge(pairs_turned, 3 * u)
                act.activation(pair_rows[:, :, D:2 * D], qk_rows[:, :, D:2 * D], ACT.Copy).then_inc(high_ready, 1)
                act.activation(pair_rows[:, :, 3 * D:4 * D], qk_rows[:, :, 0:D], ACT.Copy).then_inc(high_ready, 1)

            for u in range(2):
                turned_to_sb(u, h_turned_ps, h_turned_sb)
            feat_inputs(0)
            for u in range(2, 4):
                turned_to_sb(u, h_turned_ps, h_turned_sb)
            feat_inputs(1)
            for u in range(2):
                turned_to_sb(u, f_turned_ps, f_turned_sb)
            qk_inputs(0)
            for u in range(2, 4):
                turned_to_sb(u, f_turned_ps, f_turned_sb)
            for u in range(4):
                if u + 1 < 4:
                    qk_inputs(u + 1)
                high_halves(u)
                tiles = (1 - u // 2) * GT + u % 2 * QT
                cols = slice(tiles * P, (tiles + QT) * P)
                for m, dst in enumerate((keys[:, 0, cols], keys[:, 1, cols], queries[:, cols])):
                    act.wait_ge(pairs_turned, 3 * u + m + 1)
                    act.activation(dst, ps16[:, m, :], ACT.Copy).then_inc(pairs_stored, 1)

            act.wait_ge(z_params, 1)
            for n in range(len(L0) + 5):
                if n < len(L0):
                    act.wait_ge(z_ready, n + 1)
                    z = ps[:, 2 * (n % 3):2 * (n % 3) + 2, :]
                    act.activation(z, z, ACT.Sigmoid, scale=zscale[:, :], bias=zbias[:, :]).then_inc(sig_ready, 1)
                if n >= STEPS and n % STEPS == 2 or n == len(L0) + 2:
                    i = (n - 3) // STEPS
                    act.wait_ge(att_used, (i + 1) * STEPS)
                    act.activation(sums[:, i % 4, :], ps[:, 6 + i % 2, :], ACT.Copy).then_inc(sum_copied[0], 1)
                if n >= STEPS and n % STEPS == 4 or n == len(L0) + 4:
                    i = (n - 5) // STEPS
                    act.wait_ge(y_ready[0], i + 1)
                    if i >= 4:
                        wait_updated(act, 0, [L0_CHUNKS[i - 4]])
                    act.activation(ysb[:, i % 4], ps[:, 6 + i % 2, 0:CT * D].rearrange("p (t d) -> p t d", d=D),
                                   ACT.Copy).then_inc(y_copied[0], 1)

            for r in range(2):
                for n in range(r * len(L1) // 2, (r + 1) * len(L1) // 2):
                    if n % 2 == 0:
                        act.wait_ge(rank_ready, n + 1)
                        if n >= NW:
                            act.wait_ge(weight_used, n - NW + 1)
                        act.activation(weight_bits[:, n % NW, :], ps[:, L1[n][2] % ROUND, :], ACT.Relu)\
                           .then_inc(weight_act, 1)
                for q in range(ROUND):
                    c = r * ROUND + q
                    act.wait_ge(weight_used, (r + 1) * len(L1) // 2 - ROUND + q + 1)
                    act.activation(sums[:, q, :], ps[:, 4 + q, :], ACT.Copy).then_inc(sum_copied[1], 1)
                for q in range(ROUND):
                    c = r * ROUND + q
                    act.wait_ge(y_ready[1], c + 1)
                    if c < 4:
                        wait_updated(act, 0, L0_CHUNKS[4:])
                    else:
                        wait_updated(act, 1, [c - 4])
                    act.activation(ysb[:, c % 4], ps[:, q, 0:CT * D].rearrange("p (t d) -> p t d", d=D), ACT.Copy).then_inc(y_copied[1], 1)

            for c in range(C):
                act.wait_ge(sum_ready[2], c + 1)
                act.activation(sums[:, c % 4, :], ps[:, c % OPEN, :], ACT.Copy).then_inc(sum_copied[2], 1)
                act.wait_ge(y_ready[2], c + 1)
                if c < 4:
                    wait_updated(act, 1, [c + 4])
                else:
                    wait_updated(act, 2, [c - 4])
                act.activation(ysb[:, c % 4], ps[:, 6 + c % 2, 0:CT * D].rearrange("p (t d) -> p t d", d=D),
                               ACT.Copy).then_inc(y_copied[2], 1)

            for c in range(C):
                act.wait_ge(h3_turned_ps, c + 1)
                if c >= 2:
                    act.wait_ge(y_ready[3], c - 1)
                act.activation(h_turned[0:D, c % 2, :], ps[0:D, 6, :], ACT.Copy).then_inc(h3_turned_sb, 1)

        @block.tensor
        def _(pe):
            pe.wait_ge(scal_loaded, 16)
            pe.wait_ge(ones_set, 1)
            pe.matmul(ps[:, 7, 0:5], ones_row[:, :], scal_row[:, :], start=True, stop=True).then_inc(scal_spread, 1)
            pe.wait_ge(scal_copied, 1)

            def turn(u, ready, ps_sem, free_sem, n):
                pe.wait_ge(ready, u // 2 + 1)
                if n:
                    pe.wait_ge(free_sem, n)
                for t in range(QT):
                    at = u % 2 * QT + t
                    last = pe.transpose(ps_flat[0:D, at * P:(at + 1) * P], feat[:, (1 - u // 2) * GT + at, :], ident)
                last.then_inc(ps_sem, 1)

            def linear(u):
                pe.wait_ge(h_turned_sb, u + 1)
                for t in range(QT):
                    at = u % 2 * QT + t
                    last = pe.matmul(ps[:, 4 + u, t * D:(t + 1) * D], turned[0:D + 1, u // 2, at * P:(at + 1) * P],
                                     w0[:, :], start=t == 0, stop=True, skip_group_check=True)
                last.then_inc(lin_ready, 1)

            def linear_qk(u):
                pe.wait_ge(f_turned_sb, u + 1)
                if u < 2:
                    pe.wait_ge(feat_ready, u + 1)
                else:
                    pe.wait_ge(qk_pairs, u - 1)
                for t in range(QT):
                    b = 4 + 2 * (u % 2) + t // 4
                    last = pe.matmul(ps[:, b, (t % 4) * P:(t % 4 + 1) * P],
                                     turned[0:D + 1, u // 2, (u % 2 * QT + t) * P:(u % 2 * QT + t + 1) * P],
                                     wqk[:, :], start=t % 4 == 0, stop=True, skip_group_check=True)
                last.then_inc(qk_ready, 1)

            def turn_pairs(u):
                pe.wait_ge(qk_pairs, u + 1)
                if u == 0:
                    pe.wait_ge(f_turned_sb, 4)
                for m, at in enumerate((D, 0, 3 * D)):
                    if u:
                        pe.wait_ge(pairs_stored, 3 * (u - 1) + m + 1)
                    for t in range(QT):
                        last = pe.transpose(ps16[:, m, t * P:(t + 1) * P], pair_rows[:, t, at:at + P], ident16[:, :])
                    last.then_inc(pairs_turned, 1)

            pe.wait_ge(consts_loaded, 16)
            turn(0, h_ready, h_turned_ps, None, 0)
            turn(1, h_ready, h_turned_ps, None, 0)
            pe.wait_ge(small_loaded, 16 * 7)
            pe.wait_ge(ones_set, 3)
            linear(0)
            linear(1)
            turn(2, h_ready, h_turned_ps, h_turned_sb, 1)
            turn(3, h_ready, h_turned_ps, h_turned_sb, 2)
            linear(2)
            linear(3)
            turn(0, feat_ready, f_turned_ps, h_turned_sb, 3)
            turn(1, feat_ready, f_turned_ps, h_turned_sb, 4)
            linear_qk(0)
            turn(2, feat_ready, f_turned_ps, f_turned_sb, 1)
            turn(3, feat_ready, f_turned_ps, f_turned_sb, 2)
            linear_qk(1)
            for u in range(4):
                turn_pairs(u)
                if u + 2 < 4:
                    linear_qk(u + 2)

            def combine(layer, c, slot, bank):
                pe.wait_ge(sum_copied[layer], c + 1)
                for t in range(CT):
                    y = ps[:, bank, t * D:(t + 1) * D]
                    w = {0: both, 1: c1[:, :], 2: c2, 3: c3[:, :]}[layer]
                    last = pe.matmul(y, sums[:, slot, t * P:(t + 1) * P], w, start=t == 0, stop=layer in (0, 2),
                                     skip_group_check=True)
                    if layer == 1:
                        last = pe.matmul(y, ones_row[:, :], bias1[:, :], start=False, stop=True,
                                         skip_group_check=True)
                    if layer == 3:
                        last = pe.matmul(y, h_turned[0:D, c % 2, t * P:(t + 1) * P], w3h[:, :], start=False,
                                         stop=True, skip_group_check=True)
                last.then_inc(y_ready[layer], 1)

            LAG = 2
            for n in range(len(L0) + LAG + 4):
                if n < len(L0):
                    c, k = L0[n]
                    if n == 0:
                        pe.wait_ge(pairs_stored, 3 * T // QT)
                    if n >= 3:
                        pe.wait_ge(att_ready, n - 2)
                    for h in range(2):
                        z = ps[:, 2 * (n % 3) + h, :]
                        j = slice((2 * k + h) * P, (2 * k + h + 1) * P)
                        q = queries[:, c * CH:(c + 1) * CH]
                        pe.matmul(z, keys[:, 0, j], q, start=True, stop=False)
                        last = pe.matmul(z, keys[:, 1, j], q, start=False, stop=True)
                    last.then_inc(z_ready, 1)
                if LAG <= n < len(L0) + LAG:
                    m = n - LAG
                    c, k = L0[m]
                    i, first = m // STEPS, m % STEPS == 0
                    if first and i >= 2:
                        pe.wait_ge(y_copied[0], i - 1)
                    pe.wait_ge(att_ready, m + 1)
                    for h in range(2):
                        last = pe.matmul(ps[h * D:(h + 1) * D, 6 + i % 2, :], feat[:, 2 * k + h, :],
                                         att[:, m % 3, h * CH:(h + 1) * CH], start=first,
                                         stop=m % STEPS == STEPS - 1)
                    last.then_inc(att_used, 1)
                if n >= STEPS + LAG + 3 and (n - LAG - 3) % STEPS == 0 or n == len(L0) + LAG + 3:
                    combine(0, (n - LAG - 3) // STEPS - 1, ((n - LAG - 3) // STEPS - 1) % 4,
                            6 + ((n - LAG - 3) // STEPS - 1) % 2)

            pe.wait_ge(consts_cast, 5)
            HALF1 = len(L1) // 2
            for r in range(2):
                for s in range(HALF1 + LAG):
                    if s < HALF1:
                        n = r * HALF1 + s
                        _, b, c = L1[n]
                        q = c % ROUND
                        if r == 0 and s == 0:
                            pe.wait_ge(att_ready, len(L0))
                        if r == 1 and s < ROUND:
                            pe.wait_ge(y_copied[1], s + 1)
                        pe.matmul(ps[:, q, :], rank_w[:, :], adj8[:, c, b, :], start=b == T - 1, stop=True,
                                  skip_group_check=True).then_inc(rank_ready, 1)
                    if s >= LAG:
                        n = r * HALF1 + s - LAG
                        _, b, c = L1[n]
                        q = c % ROUND
                        if n % 2 == 0:
                            pe.wait_ge(weight_act, n // 2 + 1)
                        else:
                            pe.wait_ge(weight_dve, n // 2 + 1)
                        last = pe.matmul(ps[:, q, :], carry_w[:, :], adj8[:, c, b, :], start=False, stop=True,
                                         skip_group_check=True)
                        if b == 0:
                            last.then_inc(count_ready, 1)
                        if r == 0 and b % CT == CT - 1:
                            wait_updated(pe, 0, [b // CT])
                        if r == 0 and b == T - 1:
                            pe.wait_ge(y_copied[0], C)
                        if r == 1 and b == T - 1:
                            pe.wait_ge(sum_copied[1], ROUND)
                        last = pe.matmul(ps[:, 4 + q, :], pairs_a[:, b, :], weights[:, n % NW, :], start=b == T - 1,
                                         stop=b == 0)
                        last.then_inc(weight_used, 1)
                for q in range(ROUND):
                    if q == 0:
                        pe.wait_ge(deg_read, r * ROUND + ROUND)
                    combine(1, r * ROUND + q, q, q)

            def aggregate(layer, pairs, c, blocks, first, final):
                for b in blocks:
                    last = pe.matmul(ps[:, c % OPEN, :], pairs[:, b, :], adj8[:, c, b, :],
                                     start=first and b == blocks[0], stop=final and b == blocks[-1])
                if final:
                    last.then_inc(sum_ready[layer], 1)

            def chunk_blocks(a, b):
                return list(range(a * CT, b * CT))

            for layer, pairs in ((2, pairs_b), (3, pairs_a)):
                segments = [(0, 4), (4, 6), (6, 8)]
                for a, b in segments[:-1]:
                    wait_updated(pe, layer - 1, range(a, b))
                    for c in range(OPEN):
                        if a == 0 and layer == 2:
                            pe.wait_ge(y_copied[1], C)
                        if a == 0 and layer == 3:
                            pe.wait_ge(sum_copied[2], c + 1 + (OPEN if c < C - OPEN else 0))
                        aggregate(layer, pairs, c, chunk_blocks(a, b), a == 0, False)
                a, b = segments[-1]
                wait_updated(pe, layer - 1, range(a, b))
                for c in range(C + 1):
                    if c < C:
                        if c < OPEN:
                            aggregate(layer, pairs, c, chunk_blocks(a, b), False, True)
                        else:
                            pe.wait_ge(sum_copied[layer], c - OPEN + 1)
                            aggregate(layer, pairs, c, chunk_blocks(0, b), True, True)
                    if c >= 1:
                        m = c - 1
                        if layer == 2:
                            if m >= 2:
                                pe.wait_ge(y_copied[2], m - 1)
                            combine(2, m, m % 4, 6 + m % 2)
                        else:
                            if m == 0:
                                pe.wait_ge(y_copied[2], C)
                            for t in range(CT):
                                last = pe.transpose(ps[0:D, 6, t * P:(t + 1) * P], feat[:, m * CT + t, :], ident)
                            last.then_inc(h3_turned_ps, 1)
                            pe.wait_ge(h3_turned_sb, m + 1)
                            if m:
                                pe.wait_ge(out_ready, m)
                            combine(3, m, m % 4, 7)

        @block.vector
        def _(dve):
            do = chain(dve, dve_step)
            dve.memset(ones_row[:, :], 1.0).then_inc(ones_set, 1)
            for r in range(2):
                dve.memset(turned[D:D + 1, r, :], 1.0).then_inc(ones_set, 1)

            for g in range(2):
                tiles = slice((1 - g) * GT, (2 - g) * GT)
                X, H = x[:, tiles, :], feat[:, tiles, :]
                dve.wait_ge(x_loaded[1 - g], 16)
                do(dve.tensor_reduce(st[:, 1, 0:GT], X, AX.X, ALU.add))
                dve.scalar_tensor_tensor(H, spread(st[:, 1, 0:GT], D), -1.0 / D, X, ALU.mult, ALU.add)\
                   .then_inc(ln_centred, 1)
                dve.wait_ge(ln_squares, 2 * g + 2)
                sq = squares[:, 0, :].rearrange("p (t d) -> p t d", d=D)
                do(dve.tensor_reduce(st[:, 2, 0:GT], sq, AX.X, ALU.add))
                do(dve.tensor_scalar(st[:, 2, 0:GT], st[:, 2, 0:GT], 1.0 / D, EPS, ALU.mult, ALU.add))
                rsqrt(dve, do, st[:, 3, 0:GT], st[:, 2, 0:GT], st[:, 4, 0:GT], st[:, 5, 0:GT])
                dve.scalar_tensor_tensor(H, H, 0.0, spread(st[:, 3, 0:GT], D), ALU.max, ALU.mult)\
                   .then_inc(h_ready, 1)

            dve.wait_ge(exps_ready, 1)
            do(dve.reciprocal(zscale[:, :], scal[:, 4:5]))
            do(dve.tensor_scalar(zscale[:, :], zscale[:, :], 2.0, None, ALU.mult))
            dve.tensor_tensor(zbias[:, :], zscale[:, :], scal[:, 3:4], ALU.add).then_inc(z_params, 1)
            dve.wait_ge(small_loaded, 16 * 7)
            dve.wait_ge(consts_loaded, 16)
            dve.tensor_copy(ident16[:, :], ident).then_inc(consts_cast, 1)
            dve.tensor_copy(rank_w[:, :], rank_f32[:, 0:P]).then_inc(consts_cast, 1)
            dve.tensor_copy(carry_w[:, :], rank_f32[:, P:2 * P]).then_inc(consts_cast, 1)
            dve.tensor_scalar(c1[:, :], c1[:, :], hilo1, None, ALU.mult).then_inc(consts_cast, 1)
            dve.tensor_scalar(c3[:, :], c3[:, :], hilo3, None, ALU.mult).then_inc(consts_cast, 1)

            def sum_squares(g):
                sq = squares[:, 1 + g, :].rearrange("p (t d) -> p t d", d=D)
                dve.wait_ge(lin_acted, 2 * g + 2)
                dve.tensor_reduce(stl[:, 1, g * GT:(g + 1) * GT], sq[:, :, 1:D], AX.X, ALU.add).then_inc(lin_summed, 1)

            def features(g):
                lin = ps_flat[:, (4 + 2 * g) * CH:(6 + 2 * g) * CH].rearrange("p (t d) -> p t d", d=D)
                F = feat[:, (1 - g) * GT:(2 - g) * GT, :]
                dve.wait_ge(h_turned_ps, 2 * g + 2)
                dve.wait_ge(lin_factor, g + 1)
                do(dve.tensor_tensor(F, lin, spread(stl[:, 3, g * GT:(g + 1) * GT], D), ALU.mult))
                dve.tensor_copy(F[:, :, 0], stl[:, 0, g * GT:(g + 1) * GT]).then_inc(feat_ready, 1)

            def qk_sum_squares(u):
                sq = squares[:, u % 2, :].rearrange("p (t s d) -> p t s d", s=2, d=D)
                dve.wait_ge(qk_acted, 2 * u + 2)
                dve.tensor_reduce(stq[:, 1, u % 2, :].rearrange("p (t s) -> p t s", s=2), sq[:, :, :, 1:D],
                                  AX.X, ALU.add).then_inc(qk_summed, 1)

            def queries_keys(u):
                lin = ps_flat[:, (4 + 2 * (u % 2)) * CH:(6 + 2 * (u % 2)) * CH]\
                    .rearrange("p (t s d) -> p t s d", s=2, d=D)
                times, factors = (stq[:, k, u % 2, :].rearrange("p (t s) -> p t s", s=2) for k in (0, 3))
                rows = qk_rows.rearrange("p t (s d) -> p t s d", s=2)
                dve.wait_ge(qk_factor, u + 1)
                do(dve.tensor_tensor(rows, lin, factors.unsqueeze(3).to_broadcast([P, QT, 2, D]), ALU.mult))
                do(dve.tensor_scalar(rows[:, :, 0, 0], times[:, :, 0], -1.0, None, ALU.mult))
                dve.tensor_copy(rows[:, :, 1, 0], times[:, :, 1]).then_inc(qk_rows_ready, 1)

            def low_halves(u):
                klo, khi, klo2, qhi, qlo = (pair_rows[:, :, m * D:(m + 1) * D] for m in range(5))
                dve.wait_ge(high_ready, 2 * u + 2)
                do(dve.tensor_tensor(klo, qk_rows[:, :, D:2 * D], khi, ALU.subtract))
                do(dve.tensor_tensor(qlo, qk_rows[:, :, 0:D], qhi, ALU.subtract))
                dve.tensor_copy(klo2, klo).then_inc(qk_pairs, 1)

            sum_squares(0)
            sum_squares(1)
            features(0)
            features(1)
            qk_sum_squares(0)
            for u in range(4):
                if u + 1 < 4:
                    if u + 1 < 2:
                        qk_sum_squares(u + 1)
                queries_keys(u)
                low_halves(u)
                if 2 <= u + 2 < 4:
                    qk_sum_squares(u + 2)

            for n, (c, k) in enumerate(L0):
                dve.wait_ge(sig_ready, n + 1)
                if n < 2 * STEPS or k % (STEPS // 2) == 0:
                    dve.wait_ge(adj_loaded[c][1 if 2 * k >= HALF else 0], 16)
                if n >= 3:
                    dve.wait_ge(att_used, n - 2)
                dve.tensor_tensor(att[:, n % 3, :].rearrange("p (h i) -> p h i", h=2),
                                  ps[:, 2 * (n % 3):2 * (n % 3) + 2, :],
                                  adj8[:, c, 2 * k:2 * k + 2, :], ALU.mult).then_inc(att_ready, 1)

            for r in range(2):
                for n in range(r * len(L1) // 2, (r + 1) * len(L1) // 2):
                    if n % 2 == 1:
                        dve.wait_ge(rank_ready, n + 1)
                        if n >= NW:
                            dve.wait_ge(weight_used, n - NW + 1)
                        dve.tensor_scalar(weight_bits[:, n % NW, :], ps[:, L1[n][2] % ROUND, :], 0.0, None, ALU.max)\
                           .then_inc(weight_dve, 1)
                for q in range(ROUND):
                    c = r * ROUND + q
                    dve.wait_ge(count_ready, c + 1)
                    dve.tensor_scalar(rdeg[:, c * CH:(c + 1) * CH], ps[:, q, :], -1.0 / P, 1.0, ALU.mult, ALU.max)\
                       .then_inc(deg_read, 1)
                dve.wait_ge(deg_read, (r + 1) * ROUND)
                for q in range(ROUND):
                    c = r * ROUND + q
                    dve.reciprocal(rdeg[:, c * CH:(c + 1) * CH], rdeg[:, c * CH:(c + 1) * CH]).then_inc(deg_ready, 1)
            for layer, pairs in ((1, pairs_b), (2, pairs_a)):
                for c in BY_DVE[layer]:
                    dve.wait_ge(y_copied[layer], c + 1)
                    node_update(dve, do, layer, c, ysb[:, c % 4], st[:, :, 0:CT], tmp_v, pairs, node_dve[layer])

            dve.wait_ge(deg_ready, C)
            for c in range(C + 1):
                if c < C:
                    dve.wait_ge(sum_ready[3], c + 1)
                    if c == 0:
                        dve.wait_ge(y_ready[2], C)
                    if c >= 4:
                        dve.wait_ge(y_ready[3], c - 3)
                    dve.tensor_tensor(sums[:, c % 4, :], ps[:, c % OPEN, :], rdeg[:, c * CH:(c + 1) * CH], ALU.mult)\
                       .then_inc(sum_copied[3], 1)
                if c >= 1:
                    m = c - 1
                    dve.wait_ge(y_ready[3], m + 1)
                    X = x[:, chunk_tiles(m), :]
                    dve.scalar_tensor_tensor(X, ps[:, 7, 0:CT * D].rearrange("p (t d) -> p t d", d=D), 0.0, X,
                                             ALU.max, ALU.add).then_inc(out_ready, 1)


def kernel(**inputs):
    import numpy as np
    import concourse.bacc as bacc
    from concourse.bass_utils import run_bass_kernel_spmd

    a = {k: np.asarray(v) for k, v in inputs.items()}
    N, D = a["x"].shape
    T, C = N // 128, 8

    consts = np.zeros((128, NC_), np.float32)
    consts[:, 0:128] = np.eye(128)
    consts[:, 128:192] = np.concatenate([np.eye(D), np.eye(D) * 2.0 ** -11])
    j = np.arange(128)
    rank = 128.0 * (100.0 * np.eye(128) - (j[:, None] > j[None, :]))
    consts[:, 192:256] = np.concatenate([np.eye(D)] * 2)
    consts[:, 256] = np.where(j < D, 2.0 ** 27, 2.0 ** 16)
    consts[:, 257] = np.where(j < D, 1.0, 2.0 ** -11)

    W3 = a["L3_gnn_W"]
    arrays = {
        "x_in": np.ascontiguousarray(a["x"]),
        "adj_in": np.ascontiguousarray(
            a["adj"].T.reshape(T, 128, C, N // C).transpose(1, 2, 0, 3)).reshape(128, C, T * (N // C)),
        "w0_in": np.concatenate([a["L0_gnn_W"].T, a["L0_gnn_b"][None]]),
        "wqk_in": np.concatenate([
            np.concatenate([a["L0_gnn_Wq"].T, a["L0_gnn_bq"][None]]),
            np.concatenate([a["L0_gnn_Wk"].T, a["L0_gnn_bk"][None]])], axis=1),
        "scalars_in": np.stack([a[k] for k in (
            "L0_gnn_scale", "L0_gnn_scale_q", "L0_gnn_scale_k", "L0_gnn_att_bias", "L0_gnn_att_scale")])[None],
        "w1_in": np.concatenate([a["L1_gnn_weight"]] * 2),
        "bias1_in": a["L1_gnn_bias"][None],
        "w3h_in": np.ascontiguousarray(W3[:, :D].T),
        "w3n_in": np.concatenate([W3[:, D:].T] * 2),
        "consts_in": consts,
        "rank_in": np.concatenate([rank, -128.0 - rank], axis=1).astype(np.float32),
    }
    nc = bacc.Bacc("TRN2", target_bir_lowering=False, num_devices=1)
    args = [nc.dram_tensor(k, v.shape, mybir.dt.from_np(v.dtype), kind="ExternalInput").ap()
            for k, v in arrays.items()]
    out = nc.dram_tensor("out", (N, D), F32, kind="ExternalOutput").ap()
    gnn_program(nc, *args, out)
    r = run_bass_kernel_spmd(nc, [arrays], core_ids=[0])
    return r.results[0]["out"]
```

```python
from contextlib import ExitStack

import concourse.bass as bass
from concourse import mybir

F32 = mybir.dt.float32
F16 = mybir.dt.float16
BF16 = mybir.dt.bfloat16
F8 = mybir.dt.float8e4
I32 = mybir.dt.int32
I16 = mybir.dt.int16
ALU = mybir.AluOpType
ACT = mybir.ActivationFunctionType
AX = mybir.AxisListType

P = 128
LO = 2.0 ** 11
CUT = 100
BIAS = 127
EPS = 1e-5
TINY = 1e-8
FLT_MAX = 3.4028235e38
RSQRT_SEED = float(0x5F3759DF)
NC_ = P + 2 * 64 + 2


def gnn_program(nc, x_in, adj_in, w0_in, wqk_in, params_in, w1_in, w3h_in, w3n_in, consts_in, rank_in, out):
    N, D = x_in.shape
    T = N // P
    CH = 512
    CT = CH // P
    C = N // CH
    HALF = T // 2
    assert D == 64 and T == 32 and C == 8

    ctx = ExitStack()
    with ctx:
        def sb(name, shape, dt):
            return ctx.enter_context(nc.sbuf_tensor(name, shape, dt))

        def sem(name):
            return ctx.enter_context(nc.semaphore(name))

        adj8 = sb("adj8", [P, C, T, CH], F8)
        x = sb("x", [P, T, D], F32)
        feat = sb("feat", [P, T, D], F32)
        keys = sb("keys", [P, 2, N], F16)
        queries = sb("queries", [P, N], F16)
        att = sb("att", [P, 3, 2 * CH], F32)
        scratch = sb("scratch", [P, 5632], F32)
        consts = sb("consts", [P, NC_], F32)
        c1 = sb("c1", [P, D], F32)
        c3 = sb("c3", [P, D], F32)
        w3h = sb("w3h", [P, 2 * D], F32)
        ones_row = sb("ones_row", [1, P], F32)
        scal = sb("scal", [P, 5 + D], F32)
        exps = sb("exps", [P, 3], F32)
        zscale = sb("zscale", [P, 1], F32)
        zbias = sb("zbias", [P, 1], F32)
        warm = sb("warm", [P, 1], F32)
        ident16 = sb("ident16", [P, P], F16)
        rank_w = sb("rank_w", [P, P], BF16)
        carry_w = sb("carry_w", [P, P], BF16)
        st = sb("st", [P, 6, HALF], F32)
        stlq = sb("stlq", [P, 6 * 2 * 16], F32)
        stp = sb("stp", [P, 6, CT], F32)
        ident = consts[:, 0:P]
        c2 = consts[:, P:P + D]
        both = consts[:, P + D:P + 2 * D]
        hilo1, hilo3 = consts[:, NC_ - 2:NC_ - 1], consts[:, NC_ - 1:NC_]

        GT = HALF
        QT = 8
        pair_rows = [scratch[:, at:at + 5 * D // 2 * QT].bitcast(F16).rearrange("p (t w) -> p t w", t=QT)
                     for at in (4096, 0)]
        params = scratch[0:3, 2048:2048 + 3 * D + 2 + 5 + D]
        biases, scal_row = params[:, 0:3 * D + 2], params[0:1, 3 * D + 2:]
        bias_rest = scratch[0:3, 2368:2368 + 3 * D]
        bias_part = scratch[0:3, 2560:2560 + 3 * D // 2].bitcast(BF16)
        bias_rows = scratch[0:3, 2688:2688 + 3 * D // 2].bitcast(BF16)
        ones_rows = scratch[0:3, 2816:2816 + P // 2].bitcast(BF16)
        rank_f32 = scratch[:, 4096:4352]
        stl = scratch[:, 5376:5568].rearrange("p (k t) -> p k t", k=6)
        stq = stlq[:, :].rearrange("p (k r t) -> p k r t", k=6, r=2)
        pairs_a = scratch[:, 0:2048].bitcast(F16).rearrange("p (t w) -> p t w", t=T)
        sums = scratch[:, 2048:4096].rearrange("p (r n) -> p r n", r=4)
        ysb = scratch[:, 4096:5120].rearrange("p (r t d) -> p r t d", r=4, t=CT)
        tmp_p = scratch[:, 5120:5632].rearrange("p (r t d) -> p r t d", r=2, t=CT)
        pairs_b = queries[:, :].rearrange("p (t w) -> p t w", t=T)
        rdeg = keys[:, :, :].rearrange("p a n -> p (a n)").bitcast(F32)
        att_bytes = att[:, :, :].rearrange("p r n -> p (r n)")
        NW = 8
        weights = att_bytes[:, 0:NW * CH // 2].bitcast(BF16).rearrange("p (r n) -> p r n", r=NW)
        weight_bits = att_bytes[:, 0:NW * CH // 2].bitcast(I16).rearrange("p (r n) -> p r n", r=NW)
        LATE = 2
        late = adj8[:, 0:LATE, :, :].rearrange("p c b n -> p (c b n)").bitcast(F32)\
            .rearrange("p (r n) -> p r n", n=QT * P)
        squares = late[:, 0:3, :]
        turned = late[:, 5:7, :].rearrange("p r (h n) -> p (r h) n", h=2)
        w0 = late[:, 7, 0:2 * D]
        wqk = late[:, 7, 2 * D:6 * D]
        qk_rows = [late[:, 3 + r, :].rearrange("p (t w) -> p t w", t=QT) for r in range(2)]
        tmp_v = att_bytes[:, 2048:2560].rearrange("p (r t d) -> p r t d", r=2, t=CT)
        h_turned = att_bytes[:, 0:CH].rearrange("p (r n) -> p r n", r=2)

        ps = ctx.enter_context(nc.psum_tensor("ps", [P, 8, CH], F32))
        ps_flat = ps[:, :, :].rearrange("p b n -> p (b n)")
        ps16 = ps_flat.bitcast(F16).rearrange("p (b n) -> p b n", b=8)

        x_loaded = [sem(f"x_loaded{g}") for g in range(2)]
        small_loaded = sem("small_loaded")
        consts_loaded = sem("consts_loaded")
        params_loaded = sem("params_loaded")
        bias_split = sem("bias_split")
        warmed = sem("warmed")
        adj_loaded = [[sem(f"adj_loaded{c}_{h}") for h in range(2)] for c in range(C)]
        consts_cast = sem("consts_cast")
        ones_set = sem("ones_set")
        scal_spread = sem("scal_spread")
        scal_copied = sem("scal_copied")
        exps_ready = sem("exps_ready")
        z_params = sem("z_params")
        dve_step = sem("dve_step")
        pool_step = sem("pool_step")
        ln_squares = sem("ln_squares")
        lin_factor = sem("lin_factor")
        qk_summed = sem("qk_summed")
        qk_factor_dve = sem("qk_factor_dve")
        qk_factor_pool = sem("qk_factor_pool")
        qk_rows_ready = sem("qk_rows_ready")
        high_ready = sem("high_ready")
        ln_centred = sem("ln_centred")
        h_ready = sem("h_ready")
        h_turned_ps = sem("h_turned_ps")
        h_turned_sb = sem("h_turned_sb")
        lin_ready = sem("lin_ready")
        lin_acted = sem("lin_acted")
        feat_ready = sem("feat_ready")
        f_turned_ps = sem("f_turned_ps")
        f_turned_sb = sem("f_turned_sb")
        qk_ready = sem("qk_ready")
        qk_acted = sem("qk_acted")
        qk_pairs = sem("qk_pairs")
        pairs_turned = sem("pairs_turned")
        pairs_stored = sem("pairs_stored")
        z_ready = sem("z_ready")
        sig_ready = sem("sig_ready")
        att_ready = sem("att_ready")
        att_used = sem("att_used")
        y_copied = [sem(f"y_copied{l}") for l in range(4)]
        node_dve = [sem(f"node_dve{l}") for l in range(3)]
        node_pool = [sem(f"node_pool{l}") for l in range(3)]
        rank_ready = sem("rank_ready")
        weight_act = sem("weight_act")
        weight_dve = sem("weight_dve")
        weight_used = sem("weight_used")
        sum_ready = {l: sem(f"sum_ready{l}") for l in (2, 3)}
        sum_copied = [sem(f"sum_copied{l}") for l in range(4)]
        count_ready = sem("count_ready")
        deg_read = sem("deg_read")
        deg_ready = sem("deg_ready")
        y_ready = [sem(f"y_ready{l}") for l in range(4)]
        h3_turned_ps = sem("h3_turned_ps")
        h3_turned_sb = sem("h3_turned_sb")
        out_ready = sem("out_ready")
        out_stored = sem("out_stored")

        def chunk_tiles(c):
            return slice(c * CT, (c + 1) * CT)

        L0_CHUNKS = list(range(C))[::-1]
        STEPS = T // 2
        WIDE = STEPS + 2
        PAIR_BANK = [(0, 1, 2), (0, 1, 2), (3, 3, 3), (3, 6, 7)]
        HIGH_2, STORE_2, HIGH_3, STORE_3 = 0, [1,2,3], 4, [5,5,5]
        LOW_2, ROWS_3, LOW_3 = 0, 3, 4
        TURN_2, TURN_3 = [1,2,3], [5,5,5]
        L0 = [(c, (k + STEPS // 2) % STEPS) for c in L0_CHUNKS for k in range(STEPS)]
        Z_BANK = [(0, 4)[n % 2] if n < WIDE else (0, 4, 2)[(n - WIDE) % 3] for n in range(len(L0))]
        SUM_BANK = [2] + [6 + i % 2 for i in range(1, C)]
        ROUND = C // 2
        L1 = [(r, b, r * ROUND + q) for r in range(2) for b in range(T)[::-1] for q in range(ROUND)]
        LAG = 2
        SUM_LAG = 6
        Y_LAG = SUM_LAG + 2

        def ends_chunk(n):
            return L1[n][2] if 0 <= n < len(L1) and L1[n][1] == 0 else None
        OPEN = 6
        AHEAD = 8
        QK_POOL = [1, 3]
        BY_DVE = {0: [], 1: [4, 5, 6], 2: [0, 1, 3, 4, 6, 7]}
        BY_POOL = {0: L0_CHUNKS, 1: [0, 1, 2, 3, 7], 2: [2, 5]}

        def wait_updated(eng, layer, chunks):
            for by, done in ((BY_DVE[layer], node_dve[layer]), (BY_POOL[layer], node_pool[layer])):
                last = max([by.index(c) + 1 for c in chunks if c in by], default=0)
                if last:
                    eng.wait_ge(done, last)

        def chain(eng, counter):
            n = [0]

            def do(ins, later=False):
                n[0] += 1
                ins.then_inc(counter, 1)
                if not later:
                    eng.wait_ge(counter, n[0])
            return do

        def rsqrt(eng, do, y, v, t, vh):
            do(eng.tensor_scalar(y.bitcast(I32), v.bitcast(I32), -0.5, RSQRT_SEED, ALU.mult, ALU.add), later=True)
            do(eng.tensor_scalar(vh, v, -0.5, 1.0, ALU.mult, ALU.mult))
            for _ in range(3):
                do(eng.tensor_tensor(t, y, y, ALU.mult))
                do(eng.tensor_tensor(t, t, vh, ALU.mult))
                if eng is gpsimd:
                    do(eng.tensor_scalar(t, t, 1.0, 1.5, ALU.mult, ALU.add))
                    do(eng.tensor_tensor(y, y, t, ALU.mult))
                else:
                    do(eng.scalar_tensor_tensor(y, t, 1.5, y, ALU.add, ALU.mult))

        def lorentz_factor(eng, do, S, scale_times, done):
            scale_times(eng, do, S)
            do(eng.tensor_scalar(S[1], S[1], FLT_MAX, TINY, ALU.min, ALU.max), later=True)
            do(eng.tensor_tensor(S[2], S[0], S[0], ALU.mult))
            do(eng.tensor_scalar(S[2], S[2], 1.0, -1.0, ALU.mult, ALU.add))
            do(eng.tensor_tensor(S[1], S[1], S[2], ALU.mult))
            rsqrt(eng, do, S[3], S[1], S[4], S[5])
            eng.tensor_tensor(S[3], S[3], S[2], ALU.mult).then_inc(done, 1)

        def feature_times(eng, do, S):
            do(eng.tensor_scalar(S[0], S[0], exps[:, 0:1], 1.1, ALU.mult, ALU.add))

        def qk_times(eng, do, S):
            times = S[0].rearrange("p (t s) -> p t s", s=2)
            do(eng.tensor_tensor(times, times, exps[:, 1:3].unsqueeze(1).to_broadcast([P, QT, 2]), ALU.mult))
            do(eng.tensor_scalar(S[0], S[0], 1.0, 1.1, ALU.mult, ALU.add))

        def qk_stats(u):
            return [stq[:, k, u % 2, :] for k in range(6)]

        def row_sum(eng, do, total, v, work):
            if eng is not gpsimd:
                do(eng.tensor_reduce(total, v, AX.X, ALU.add))
                return
            width = D // 2
            do(eng.tensor_tensor(work[:, :, 0:width], v[:, :, 0:width], v[:, :, width:D], ALU.add))
            while width > 2:
                width //= 2
                do(eng.tensor_tensor(work[:, :, 0:width], work[:, :, 0:width], work[:, :, width:2 * width], ALU.add))
            do(eng.tensor_tensor(total, work[:, :, 0], work[:, :, 1], ALU.add))

        def spread(v, n):
            return v.unsqueeze(2).to_broadcast([P, v.shape[1], n])

        def node_update(eng, do, layer, c, y, s, tmp, pairs, done):
            on_dve = eng is not gpsimd
            tiles = chunk_tiles(c)
            X, H = x[:, tiles, :], feat[:, tiles, :]
            a, b = tmp[:, 0], tmp[:, 1]
            if layer == 0:
                do(eng.tensor_tensor(a, y, y, ALU.mult))
                do(eng.tensor_scalar(a[:, :, 0], a[:, :, 0], -1.0, 1.0, ALU.mult, ALU.mult))
                row_sum(eng, do, s[:, 0], a, a)
                do(eng.tensor_scalar(s[:, 1], s[:, 0], -1.0, 0.0, ALU.mult, ALU.max))
                do(eng.tensor_scalar(s[:, 0], s[:, 0], FLT_MAX, 0.0, ALU.min, ALU.max))
                do(eng.tensor_tensor(s[:, 0], s[:, 0], s[:, 1], ALU.add))
                do(eng.tensor_scalar(s[:, 0], s[:, 0], FLT_MAX, TINY, ALU.min, ALU.max))
                rsqrt(eng, do, s[:, 1], s[:, 0], s[:, 2], s[:, 3])
                do(eng.tensor_tensor(a, y, spread(s[:, 1], D), ALU.mult))
                do(eng.tensor_tensor(X, X, a, ALU.add))
            elif layer == 1:
                do(eng.tensor_tensor(X, X, y, ALU.add))
            else:
                do(eng.tensor_tensor(a, H, y, ALU.mult))
                row_sum(eng, do, s[:, 0], a, a)
                do(eng.tensor_scalar(s[:, 0], s[:, 0], -0.01, 1.0, ALU.mult, ALU.add))
                if on_dve:
                    do(eng.scalar_tensor_tensor(X, H, -0.1, X, ALU.mult, ALU.add))
                    do(eng.tensor_tensor(X, X, spread(s[:, 0], D), ALU.add))
                else:
                    do(eng.tensor_scalar(b, H, -0.1, 1.0, ALU.mult, ALU.mult))
                    do(eng.tensor_tensor(b, b, spread(s[:, 0], D), ALU.add))
                    do(eng.tensor_tensor(X, X, b, ALU.add))
            row_sum(eng, do, s[:, 0], X, a)
            if on_dve:
                do(eng.scalar_tensor_tensor(a, spread(s[:, 0], D), -1.0 / D, X, ALU.mult, ALU.add))
            else:
                do(eng.tensor_scalar(s[:, 0], s[:, 0], -1.0 / D, 1.0, ALU.mult, ALU.mult))
                do(eng.tensor_tensor(a, X, spread(s[:, 0], D), ALU.add))
            do(eng.tensor_tensor(b, a, a, ALU.mult))
            row_sum(eng, do, s[:, 1], b, b)
            do(eng.tensor_scalar(s[:, 1], s[:, 1], 1.0 / D, EPS, ALU.mult, ALU.add))
            rsqrt(eng, do, s[:, 2], s[:, 1], s[:, 3], s[:, 4])
            h = H if layer > 0 else b
            if on_dve:
                do(eng.scalar_tensor_tensor(h, a, 0.0, spread(s[:, 2], D), ALU.max, ALU.mult))
            else:
                do(eng.tensor_scalar(a, a, FLT_MAX, 0.0, ALU.min, ALU.max))
                do(eng.tensor_tensor(h, a, spread(s[:, 2], D), ALU.mult))
            hi, lo = pairs[:, tiles, 0:D], pairs[:, tiles, D:2 * D]
            do(eng.tensor_scalar(hi, h, 1.0, 1.0, ALU.mult, ALU.mult))
            do(eng.tensor_tensor(a, h, hi, ALU.subtract))
            if layer == 0:
                do(eng.tensor_tensor(X, X, scal[:, 5:5 + D].unsqueeze(1).to_broadcast([P, CT, D]), ALU.add))
            eng.tensor_scalar(lo, a, LO, 1.0, ALU.mult, ALU.mult).then_inc(done, 1)
            eng.wait_ge(done, (BY_DVE if on_dve else BY_POOL)[layer].index(c) + 1)

        gpsimd = nc.gpsimd
        block = ctx.enter_context(nc.Block())

        @block.sync
        def _(sp):
            xr = x_in.rearrange("(t p) d -> p t d", p=P)
            for g in (1, 0):
                sp.dma_start(x[:, g * GT:(g + 1) * GT, :], xr[:, g * GT:(g + 1) * GT, :]).then_inc(x_loaded[g], 16)
            for dst, src in ((w0, w0_in), (wqk, wqk_in), (rank_f32, rank_in), (c1[:, :], w1_in),
                             (w3h[:, :], w3h_in), (c3[:, :], w3n_in)):
                sp.dma_start(dst, src).then_inc(small_loaded, 16)
            outr = out.rearrange("(t p) d -> p t d", p=P)
            for c in range(C):
                sp.wait_ge(out_ready, c + 1)
                sp.dma_start(outr[:, chunk_tiles(c), :], x[:, chunk_tiles(c), :]).then_inc(out_stored, 16)
            sp.wait_ge(out_stored, 16 * C)

        @block.gpsimd
        def _(pool):
            def load(chunks):
                for c in chunks:
                    for h in (1, 0):
                        dst = adj8[:, c, h * HALF:(h + 1) * HALF, :].rearrange("p b n -> p (b n)")
                        src = adj_in[:, c, h * HALF * CH:(h + 1) * HALF * CH]
                        pool.dma_start(dst, src, max_dma_last_dim=2048).then_inc(adj_loaded[c][h], 16)

            load(L0_CHUNKS[:-LATE])
            assert pool is gpsimd
            do = chain(pool, pool_step)

            pool.wait_ge(exps_ready, 1)
            for u in QK_POOL:
                pool.wait_ge(qk_summed, u + 1)
                lorentz_factor(pool, do, qk_stats(u), qk_times, qk_factor_pool)

            pool.wait_ge(pairs_stored, 3 * T // QT)
            load(L0_CHUNKS[-LATE:])
            for layer, pairs in ((0, pairs_a), (1, pairs_b), (2, pairs_a)):
                for c in BY_POOL[layer]:
                    n = L0_CHUNKS.index(c) if layer == 0 else c
                    pool.wait_ge(y_copied[layer], n + 1)
                    node_update(pool, do, layer, c, ysb[:, n % 4], stp, tmp_p, pairs, node_pool[layer])

        @block.scalar
        def _(act):
            act.dma_start(params, params_in).then_inc(params_loaded, 16)
            act.dma_start(consts[:, :], consts_in).then_inc(consts_loaded, 16)
            act.wait_ge(scal_spread, 1)
            act.activation(scal[:, :], ps[:, 7, 0:5 + D], ACT.Copy).then_inc(scal_copied, 1)
            act.wait_ge(scal_copied, 1)
            act.activation(exps[:, :], scal[:, 0:3], ACT.Exp).then_inc(exps_ready, 1)
            act.wait_ge(exps_ready, 1)
            act.activation(warm[:, :], scal[:, 0:1], ACT.Sigmoid).then_inc(warmed, 1)
            for g in range(2):
                act.wait_ge(ln_centred, g + 1)
                for q in range(2):
                    tiles = slice((1 - g) * GT + q * QT, (1 - g) * GT + (q + 1) * QT)
                    act.activation(squares[:, g, q * QT * D:(q + 1) * QT * D].rearrange("p (t d) -> p t d", d=D),
                                   feat[:, tiles, :], ACT.Square).then_inc(ln_squares, 1)

            def turned_to_sb(u, ps_sem, sb_sem):
                act.wait_ge(ps_sem, u + 1)
                act.activation(turned[:, u, :], ps[:, u, :], ACT.Copy).then_inc(sb_sem, 1)

            def lorentz_inputs(view, sq, times, ready, n, acted):
                act.wait_ge(ready, n + 1)
                act.activation(times, view[..., 0], ACT.Sigmoid).then_inc(acted, 1)
                act.activation(sq, view, ACT.Square).then_inc(acted, 1)

            def feat_inputs(g):
                lin = ps_flat[:, (4 + 2 * g) * CH:(6 + 2 * g) * CH].rearrange("p (t d) -> p t d", d=D)
                lorentz_inputs(lin, squares[:, (2 + g) % 3, :].rearrange("p (t d) -> p t d", d=D),
                               stl[:, 0, g * GT:(g + 1) * GT], lin_ready, 2 * g + 1, lin_acted)

            def qk_inputs(u):
                if u >= 2:
                    act.wait_ge(qk_rows_ready, u - 1)
                lin = ps_flat[:, (4 + 2 * (u % 2)) * CH:(6 + 2 * (u % 2)) * CH]
                lorentz_inputs(lin.rearrange("p (t s d) -> p t s d", s=2, d=D),
                               squares[:, (u + 1) % 2, :].rearrange("p (t s d) -> p t s d", s=2, d=D),
                               stq[:, 0, u % 2, :].rearrange("p (t s) -> p t s", s=2),
                               qk_ready, u, qk_acted)

            def high_halves(u):
                act.wait_ge(qk_rows_ready, u + 1)
                if u >= 2:
                    act.wait_ge(pairs_turned, 3 * (u - 1))
                rows = pair_rows[u % 2]
                act.activation(rows[:, :, D:2 * D], qk_rows[u % 2][:, :, D:2 * D], ACT.Copy).then_inc(high_ready, 1)
                act.activation(rows[:, :, 3 * D:4 * D], qk_rows[u % 2][:, :, 0:D], ACT.Copy).then_inc(high_ready, 1)

            def store_pairs(u, pieces=(0, 1, 2)):
                tiles = (1 - u // 2) * GT + u % 2 * QT
                cols = slice(tiles * P, (tiles + QT) * P)
                for m in pieces:
                    dst = (keys[:, 0, cols], keys[:, 1, cols], queries[:, cols])[m]
                    act.wait_ge(pairs_turned, 3 * u + m + 1)
                    act.activation(dst, ps16[:, PAIR_BANK[u][m], :], ACT.Copy).then_inc(pairs_stored, 1)

            for u in range(2):
                turned_to_sb(u, h_turned_ps, h_turned_sb)
            feat_inputs(0)
            for u in range(2, 4):
                turned_to_sb(u, h_turned_ps, h_turned_sb)
            feat_inputs(1)
            for u in range(2):
                turned_to_sb(u, f_turned_ps, f_turned_sb)
            qk_inputs(0)
            for u in range(2, 4):
                turned_to_sb(u, f_turned_ps, f_turned_sb)
            qk_inputs(1)
            high_halves(0)
            qk_inputs(2)
            store_pairs(0)
            high_halves(1)
            qk_inputs(3)
            store_pairs(1)

            act.wait_ge(z_params, 1)
            for n in range(len(L0) + 5):
                if n < len(L0):
                    act.wait_ge(z_ready, n + 1)
                    z = ps[:, Z_BANK[n]:Z_BANK[n] + 2, :]
                    act.activation(z, z, ACT.Sigmoid, scale=zscale[:, :], bias=zbias[:, :]).then_inc(sig_ready, 1)
                if n == HIGH_2:
                    high_halves(2)
                if n in STORE_2:
                    store_pairs(2, [m for m in range(3) if STORE_2[m] == n])
                if n == HIGH_3:
                    high_halves(3)
                if n in STORE_3:
                    store_pairs(3, [m for m in range(3) if STORE_3[m] == n])
                if n >= STEPS and n % STEPS == 2 or n == len(L0) + 2:
                    i = (n - 3) // STEPS
                    act.wait_ge(att_used, (i + 1) * STEPS)
                    act.activation(sums[:, i % 4, :], ps[:, SUM_BANK[i], :], ACT.Copy).then_inc(sum_copied[0], 1)
                if n >= STEPS and n % STEPS == 4 or n == len(L0) + 4:
                    i = (n - 5) // STEPS
                    act.wait_ge(y_ready[0], i + 1)
                    if i >= 4:
                        wait_updated(act, 0, [L0_CHUNKS[i - 4]])
                    act.activation(ysb[:, i % 4], ps[:, 6 + i % 2, 0:CT * D].rearrange("p (t d) -> p t d", d=D),
                                   ACT.Copy).then_inc(y_copied[0], 1)

            for s in range(len(L1) + Y_LAG + 1):
                if s < len(L1) and s % 2 == 0:
                    act.wait_ge(rank_ready, s + 1)
                    if s >= NW:
                        act.wait_ge(weight_used, s - NW + 1)
                    act.activation(weight_bits[:, s % NW, :], ps[:, L1[s][2] % ROUND, :], ACT.Relu)\
                       .then_inc(weight_act, 1)
                c = ends_chunk(s - SUM_LAG)
                if c is not None:
                    act.wait_ge(weight_used, s - SUM_LAG + 1)
                    act.activation(sums[:, c % 4, :], ps[:, 4 + c % ROUND, :], ACT.Copy).then_inc(sum_copied[1], 1)
                c = ends_chunk(s - Y_LAG)
                if c is not None:
                    act.wait_ge(y_ready[1], c + 1)
                    if c < 4:
                        wait_updated(act, 0, L0_CHUNKS[4:])
                    else:
                        wait_updated(act, 1, [c - 4])
                    act.activation(ysb[:, c % 4], ps[:, 4 + c % ROUND, 0:CT * D].rearrange("p (t d) -> p t d", d=D),
                                   ACT.Copy).then_inc(y_copied[1], 1)

            for c in range(C):
                act.wait_ge(sum_ready[2], c + 1)
                act.activation(sums[:, c % 4, :], ps[:, c % OPEN, :], ACT.Copy).then_inc(sum_copied[2], 1)
                act.wait_ge(y_ready[2], c + 1)
                if c < 4:
                    wait_updated(act, 1, [c + 4])
                else:
                    wait_updated(act, 2, [c - 4])
                act.activation(ysb[:, c % 4], ps[:, 6 + c % 2, 0:CT * D].rearrange("p (t d) -> p t d", d=D),
                               ACT.Copy).then_inc(y_copied[2], 1)

            for c in range(C):
                act.wait_ge(h3_turned_ps, c + 1)
                if c >= 2:
                    act.wait_ge(y_ready[3], c - 1)
                act.activation(h_turned[:, c % 2, :], ps[:, 6, 0:CH // 2], ACT.Copy).then_inc(h3_turned_sb, 1)

        @block.tensor
        def _(pe):
            pe.wait_ge(params_loaded, 16)
            pe.wait_ge(ones_set, 1)
            pe.matmul(ps[:, 7, 0:5 + D], ones_row[:, :], scal_row, start=True, stop=True).then_inc(scal_spread, 1)
            pe.wait_ge(scal_copied, 1)

            def stay_warm(times):
                for _ in range(times):
                    pe.transpose(ps[:, 3, 0:P], ident, ident)

            def turn(u, ready, ps_sem, free_sem, n):
                pe.wait_ge(ready, u // 2 + 1)
                if n:
                    pe.wait_ge(free_sem, n)
                tile = (1 - u // 2) * GT + u % 2 * QT
                for t in range(0, QT, 2):
                    last = pe.transpose(ps[:, u, t * D:(t + 2) * D],
                                        feat[:, tile + t:tile + t + 2, :].rearrange("p t d -> p (t d)"), ident)
                last.then_inc(ps_sem, 1)

            def bias(bank, which):
                v = (bias_rows[:, 0:D], bias_rows[:, D:3 * D])[which].unsqueeze(1)
                pe.matmul(ps[:, bank, :].rearrange("p (t w) -> p t w", w=v.shape[2]), ones_rows,
                          v.to_broadcast([3, CH // v.shape[2], v.shape[2]]), start=True, stop=False,
                          skip_group_check=True)

            def linear(u):
                pe.wait_ge(h_turned_sb, u + 1)
                for t in range(0, QT, 2):
                    last = pe.matmul(ps[:, 4 + u, t * D:(t + 2) * D], turned[:, u, t * D:(t + 2) * D],
                                     w0, start=False, stop=True, skip_group_check=True)
                last.then_inc(lin_ready, 1)

            def bias_qk(u):
                if u < 2:
                    pe.wait_ge(feat_ready, u + 1)
                else:
                    pe.wait_ge(qk_rows_ready, u - 1)
                for h in range(2):
                    bias(4 + 2 * (u % 2) + h, 1)

            def linear_qk(u):
                pe.wait_ge(f_turned_sb, u + 1)
                for t in range(0, QT, 2):
                    last = pe.matmul(ps[:, 4 + 2 * (u % 2) + t // 4, t % 4 * P:(t % 4 + 2) * P],
                                     turned[:, u, t * D:(t + 2) * D], wqk, start=False, stop=True,
                                     skip_group_check=True)
                last.then_inc(qk_ready, 1)

            def turn_pairs(u, pieces=(0, 1, 2)):
                pe.wait_ge(qk_pairs, u + 1)
                if u == 0:
                    pe.wait_ge(f_turned_sb, 4)
                for m in pieces:
                    before = [3 * v + k for v in range(4) for k in range(3)
                              if (v, k) < (u, m) and PAIR_BANK[v][k] == PAIR_BANK[u][m]]
                    if before:
                        pe.wait_ge(pairs_stored, before[-1] + 1)
                    at = (D, 0, 3 * D)[m]
                    for t in range(QT):
                        last = pe.transpose(ps16[:, PAIR_BANK[u][m], t * P:(t + 1) * P],
                                            pair_rows[u % 2][:, t, at:at + P], ident16[:, :])
                    last.then_inc(pairs_turned, 1)

            pe.wait_ge(bias_split, 1)
            for u in range(4):
                bias(4 + u, 0)
            pe.wait_ge(consts_loaded, 16)
            stay_warm(8)
            for u in (0, 1):
                turn(u, h_ready, h_turned_ps, None, 0)
            pe.wait_ge(small_loaded, 16 * 6)
            linear(0)
            linear(1)
            for u in (2, 3):
                turn(u, h_ready, h_turned_ps, None, 0)
            linear(2)
            linear(3)
            stay_warm(9)
            for g in range(2):
                for u in (2 * g, 2 * g + 1):
                    turn(u, feat_ready, f_turned_ps, h_turned_sb, u + 1)
                bias_qk(g)
                linear_qk(g)
                if g == 0:
                    stay_warm(6)
            pe.wait_ge(f_turned_sb, 4)
            stay_warm(14)
            bias_qk(2)
            linear_qk(2)
            turn_pairs(0)
            stay_warm(8)
            bias_qk(3)
            linear_qk(3)
            stay_warm(4)
            turn_pairs(1)
            stay_warm(12)

            def combine(layer, c, slot, bank):
                if layer == 3:
                    for t in range(0, CT, 2):
                        pe.matmul(ps[:, bank, t * D:(t + 2) * D], h_turned[:, c % 2, t * D:(t + 2) * D], w3h[:, :],
                                  start=t == 0, stop=False, skip_group_check=True)
                w = {0: both, 1: c1[:, :], 2: c2, 3: c3[:, :]}[layer]
                pe.wait_ge(sum_copied[layer], c + 1)
                for t in range(CT):
                    last = pe.matmul(ps[:, bank, t * D:(t + 1) * D], sums[:, slot, t * P:(t + 1) * P], w,
                                     start=layer != 3 and t == 0, stop=True, skip_group_check=True)
                last.then_inc(y_ready[layer], 1)

            for n in range(len(L0) + LAG + 4):
                if n < len(L0):
                    c, k = L0[n]
                    if n == 0:
                        pe.wait_ge(pairs_stored, 3 * 2)
                    elif n == 1:
                        pe.wait_ge(qk_rows_ready, 3)
                    elif Z_BANK[n] not in Z_BANK[:n]:
                        pe.wait_ge(sum_copied[0], 1)
                    else:
                        pe.wait_ge(att_ready, max(m for m in range(n) if Z_BANK[m] == Z_BANK[n]) + 1)
                    if n == STEPS // 2:
                        pe.wait_ge(pairs_stored, 3 * 4)
                    for h in range(2):
                        z = ps[:, Z_BANK[n] + h, :]
                        j = slice((2 * k + h) * P, (2 * k + h + 1) * P)
                        q = queries[:, c * CH:(c + 1) * CH]
                        pe.matmul(z, keys[:, 0, j], q, start=True, stop=False)
                        last = pe.matmul(z, keys[:, 1, j], q, start=False, stop=True)
                    last.then_inc(z_ready, 1)
                if n in TURN_2:
                    turn_pairs(2, [m for m in range(3) if TURN_2[m] == n])
                if n in TURN_3:
                    turn_pairs(3, [m for m in range(3) if TURN_3[m] == n])
                if LAG <= n < len(L0) + LAG:
                    m = n - LAG
                    c, k = L0[m]
                    i, first = m // STEPS, m % STEPS == 0
                    if first and i >= 2:
                        pe.wait_ge(y_copied[0], i - 1)
                    pe.wait_ge(att_ready, m + 1)
                    for h in range(2):
                        last = pe.matmul(ps[h * D:(h + 1) * D, SUM_BANK[i], :], feat[:, 2 * k + h, :],
                                         att[:, m % 3, h * CH:(h + 1) * CH], start=first,
                                         stop=m % STEPS == STEPS - 1)
                    last.then_inc(att_used, 1)
                if n >= STEPS + LAG + 3 and (n - LAG - 3) % STEPS == 0 or n == len(L0) + LAG + 3:
                    combine(0, (n - LAG - 3) // STEPS - 1, ((n - LAG - 3) // STEPS - 1) % 4,
                            6 + ((n - LAG - 3) // STEPS - 1) % 2)

            def aggregate(layer, pairs, c, blocks, first, final):
                for b in blocks:
                    last = pe.matmul(ps[:, c % OPEN, :], pairs[:, b, :], adj8[:, c, b, :],
                                     start=first and b == blocks[0], stop=final and b == blocks[-1])
                if final:
                    last.then_inc(sum_ready[layer], 1)

            def chunk_blocks(a, b):
                return list(range(a * CT, b * CT))

            pe.wait_ge(consts_cast, 5)
            for s in range(len(L1) + Y_LAG):
                if s < len(L1):
                    r, b, c = L1[s]
                    if s == 0:
                        pe.wait_ge(att_ready, len(L0))
                    if r == 1 and b == T - 1:
                        pe.wait_ge(deg_read, c % ROUND + 1)
                    pe.matmul(ps[:, c % ROUND, :], rank_w[:, :], adj8[:, c, b, :], start=b == T - 1, stop=True,
                              skip_group_check=True).then_inc(rank_ready, 1)
                if LAG <= s < len(L1) + LAG:
                    n = s - LAG
                    _, b, c = L1[n]
                    pe.wait_ge(weight_dve if n % 2 else weight_act, n // 2 + 1)
                    last = pe.matmul(ps[:, c % ROUND, :], carry_w[:, :], adj8[:, c, b, :], start=False, stop=True,
                                     skip_group_check=True)
                    if b == 0:
                        last.then_inc(count_ready, 1)
                if s == len(L1) + SUM_LAG:
                    pe.wait_ge(deg_read, ROUND + 1)
                    wait_updated(pe, 1, range(0, AHEAD // CT))
                    aggregate(2, pairs_b, 0, range(AHEAD), True, False)
                if ends_chunk(s - Y_LAG) is not None:
                    c = ends_chunk(s - Y_LAG)
                    combine(1, c, c % 4, 4 + c % ROUND)
                if SUM_LAG <= s < len(L1) + SUM_LAG:
                    n = s - SUM_LAG
                    r, b, c = L1[n]
                    if r == 0 and b % CT == CT - 1:
                        wait_updated(pe, 0, [b // CT])
                    if r == 0 and b == T - 1:
                        pe.wait_ge(y_copied[0], C)
                    if r == 1 and b == T - 1:
                        pe.wait_ge(y_copied[1], c % ROUND + 1)
                    pe.matmul(ps[:, 4 + c % ROUND, :], pairs_a[:, b, :], weights[:, n % NW, :], start=b == T - 1,
                              stop=b == 0).then_inc(weight_used, 1)

            for layer, pairs in ((2, pairs_b), (3, pairs_a)):
                segments = [(0, 4), (4, 5), (5, 6), (6, 7), (7, 8)] if layer == 2 else \
                    [(0, 2), (2, 3), (3, 4), (4, 5), (5, 6), (6, 7), (7, 8)]
                for a, b in segments[:-1]:
                    wait_updated(pe, layer - 1, range(a, b))
                    for c in range(OPEN):
                        if a == 0 and layer == 2 and c < ROUND:
                            pe.wait_ge(deg_read, ROUND + c + 1)
                        if a == 0 and layer == 2 and c >= ROUND:
                            pe.wait_ge(y_copied[1], c + 1)
                        if a == 0 and layer == 3:
                            pe.wait_ge(sum_copied[2], c + 1 + (OPEN if c < C - OPEN else 0))
                        if a == 0 and layer == 2 and c == 0:
                            aggregate(layer, pairs, c, range(AHEAD, b * CT), False, False)
                        else:
                            aggregate(layer, pairs, c, chunk_blocks(a, b), a == 0, False)
                a, b = segments[-1]
                wait_updated(pe, layer - 1, range(a, b))
                for c in range(C + 1):
                    if c < OPEN:
                        aggregate(layer, pairs, c, chunk_blocks(a, b), False, True)
                    elif c < C:
                        pe.wait_ge(sum_copied[layer], c - OPEN + 1)
                        aggregate(layer, pairs, c, chunk_blocks(0, b), True, True)
                    if layer == 3 and c < C:
                        if c == 0:
                            pe.wait_ge(y_copied[2], C)
                        else:
                            pe.wait_ge(h3_turned_sb, c)
                        for t in range(0, CT, 2):
                            last = pe.transpose(ps[:, 6, t * D:(t + 2) * D],
                                                feat[:, c * CT + t:c * CT + t + 2, :].rearrange("p t d -> p (t d)"), ident)
                        last.then_inc(h3_turned_ps, 1)
                    if c >= 1:
                        m = c - 1
                        if layer == 2 and m < 2:
                            pe.wait_ge(y_copied[1], C)
                        if layer == 2 and m >= 2:
                            pe.wait_ge(y_copied[2], m - 1)
                        if layer == 3:
                            pe.wait_ge(h3_turned_sb, m + 1)
                            if m:
                                pe.wait_ge(out_ready, m)
                        combine(layer, m, m % 4, 7 if layer == 3 else 6 + m % 2)

        @block.vector
        def _(dve):
            do = chain(dve, dve_step)
            dve.memset(ones_row[:, :], 1.0).then_inc(ones_set, 1)
            dve.memset(ones_rows, 1.0).then_inc(ones_set, 1)

            def rows_of(g):
                tiles = slice((1 - g) * GT, (2 - g) * GT)
                return x[:, tiles, :], feat[:, tiles, :]

            def x_sum(g):
                dve.wait_ge(x_loaded[1 - g], 16)
                do(dve.tensor_reduce(stl[:, g, 0:GT], rows_of(g)[0], AX.X, ALU.add))

            def centre(g):
                X, H = rows_of(g)
                dve.scalar_tensor_tensor(H, spread(stl[:, g, 0:GT], D), -1.0 / D, X, ALU.mult, ALU.add)\
                   .then_inc(ln_centred, 1)

            def variance(g):
                dve.wait_ge(ln_squares, 2 * g + 2)
                sq = squares[:, g, :].rearrange("p (t d) -> p t d", d=D)
                do(dve.tensor_reduce(st[:, 2, :], sq, AX.X, ALU.add))
                do(dve.tensor_scalar(st[:, 2, :], st[:, 2, :], 1.0 / D, EPS, ALU.mult, ALU.add))

            def normalise(g):
                rsqrt(dve, do, st[:, 3, :], st[:, 2, :], st[:, 4, :], st[:, 5, :])
                H = rows_of(g)[1]
                dve.wait_ge(ln_centred, g + 1)
                dve.scalar_tensor_tensor(H, H, 0.0, spread(st[:, 3, :], D), ALU.max, ALU.mult)\
                   .then_inc(h_ready, 1)

            x_sum(0)
            centre(0)
            dve.wait_ge(params_loaded, 16)
            do(dve.tensor_copy(bias_part, biases[:, 0:3 * D]))
            do(dve.scalar_tensor_tensor(bias_rest, bias_part, biases[:, 3 * D:3 * D + 1], biases[:, 0:3 * D],
                                        ALU.mult, ALU.add))
            do(dve.tensor_copy(bias_part, bias_rest), later=True)
            x_sum(1)
            dve.scalar_tensor_tensor(bias_rows, bias_part, biases[:, 3 * D + 1:3 * D + 2], bias_rest,
                                     ALU.mult, ALU.add).then_inc(bias_split, 1)
            variance(0)
            centre(1)
            normalise(0)
            dve.wait_ge(h_ready, 1)
            variance(1)
            normalise(1)

            dve.wait_ge(exps_ready, 1)
            do(dve.reciprocal(zscale[:, :], scal[:, 4:5]))
            do(dve.tensor_scalar(zscale[:, :], zscale[:, :], 2.0, None, ALU.mult))
            dve.tensor_tensor(zbias[:, :], zscale[:, :], scal[:, 3:4], ALU.add).then_inc(z_params, 1)
            dve.wait_ge(small_loaded, 16 * 6)
            dve.wait_ge(consts_loaded, 16)
            dve.tensor_copy(ident16[:, :], ident).then_inc(consts_cast, 1)
            dve.tensor_copy(rank_w[:, :], rank_f32[:, 0:P]).then_inc(consts_cast, 1)
            dve.tensor_copy(carry_w[:, :], rank_f32[:, P:2 * P]).then_inc(consts_cast, 1)
            dve.tensor_scalar(c1[:, :], c1[:, :], hilo1, None, ALU.mult).then_inc(consts_cast, 1)
            dve.tensor_scalar(c3[:, :], c3[:, :], hilo3, None, ALU.mult).then_inc(consts_cast, 1)

            def feature_stats(g):
                return [stl[:, k, g * GT:(g + 1) * GT] for k in range(6)]

            def sum_squares(g):
                sq = squares[:, (2 + g) % 3, :].rearrange("p (t d) -> p t d", d=D)
                dve.wait_ge(lin_acted, 2 * g + 2)
                do(dve.tensor_reduce(feature_stats(g)[1], sq[:, :, 1:D], AX.X, ALU.add))
                lorentz_factor(dve, do, feature_stats(g), feature_times, lin_factor)
                dve.wait_ge(lin_factor, g + 1)

            def features(g):
                lin = ps_flat[:, (4 + 2 * g) * CH:(6 + 2 * g) * CH].rearrange("p (t d) -> p t d", d=D)
                F = feat[:, (1 - g) * GT:(2 - g) * GT, :]
                dve.wait_ge(h_turned_ps, 2 * g + 2)
                do(dve.tensor_tensor(F, lin, spread(stl[:, 3, g * GT:(g + 1) * GT], D), ALU.mult))
                dve.tensor_copy(F[:, :, 0], stl[:, 0, g * GT:(g + 1) * GT]).then_inc(feat_ready, 1)

            def qk_sum_squares(u):
                sq = squares[:, (u + 1) % 2, :].rearrange("p (t s d) -> p t s d", s=2, d=D)
                dve.wait_ge(qk_acted, 2 * u + 2)
                dve.tensor_reduce(stq[:, 1, u % 2, :].rearrange("p (t s) -> p t s", s=2), sq[:, :, :, 1:D],
                                  AX.X, ALU.add).then_inc(qk_summed, 1)

            def queries_keys(u):
                lin = ps_flat[:, (4 + 2 * (u % 2)) * CH:(6 + 2 * (u % 2)) * CH]\
                    .rearrange("p (t s d) -> p t s d", s=2, d=D)
                times, factors = (stq[:, k, u % 2, :].rearrange("p (t s) -> p t s", s=2) for k in (0, 3))
                rows = qk_rows[u % 2].rearrange("p t (s d) -> p t s d", s=2)
                if u in QK_POOL:
                    dve.wait_ge(qk_factor_pool, QK_POOL.index(u) + 1)
                else:
                    lorentz_factor(dve, do, qk_stats(u), qk_times, qk_factor_dve)
                    dve.wait_ge(qk_factor_dve, u // 2 + 1)
                do(dve.tensor_tensor(rows, lin, factors.unsqueeze(3).to_broadcast([P, QT, 2, D]), ALU.mult))
                do(dve.tensor_scalar(rows[:, :, 0, 0], times[:, :, 0], -1.0, None, ALU.mult))
                dve.tensor_copy(rows[:, :, 1, 0], times[:, :, 1]).then_inc(qk_rows_ready, 1)

            def low_halves(u):
                klo, khi, klo2, qhi, qlo = (pair_rows[u % 2][:, :, m * D:(m + 1) * D] for m in range(5))
                dve.wait_ge(high_ready, 2 * u + 2)
                do(dve.tensor_tensor(klo, qk_rows[u % 2][:, :, D:2 * D], khi, ALU.subtract), later=True)
                do(dve.tensor_tensor(qlo, qk_rows[u % 2][:, :, 0:D], qhi, ALU.subtract))
                dve.tensor_copy(klo2, klo).then_inc(qk_pairs, 1)

            for g in range(2):
                sum_squares(g)
                features(g)
            qk_sum_squares(0)
            queries_keys(0)
            qk_sum_squares(1)
            low_halves(0)
            qk_sum_squares(2)
            queries_keys(1)
            low_halves(1)
            queries_keys(2)
            qk_sum_squares(3)

            for n, (c, k) in enumerate(L0):
                dve.wait_ge(sig_ready, n + 1)
                if n < 2 * STEPS or k % (STEPS // 2) == 0:
                    dve.wait_ge(adj_loaded[c][1 if 2 * k >= HALF else 0], 16)
                if n >= 3:
                    dve.wait_ge(att_used, n - 2)
                dve.tensor_tensor(att[:, n % 3, :].rearrange("p (h i) -> p h i", h=2),
                                  ps[:, Z_BANK[n]:Z_BANK[n] + 2, :],
                                  adj8[:, c, 2 * k:2 * k + 2, :], ALU.mult).then_inc(att_ready, 1)
                if n == LOW_2:
                    low_halves(2)
                if n == ROWS_3:
                    queries_keys(3)
                if n == LOW_3:
                    low_halves(3)

            for s in range(len(L1) + LAG):
                if s < len(L1) and s % 2 == 1:
                    dve.wait_ge(rank_ready, s + 1)
                    if s >= NW:
                        dve.wait_ge(weight_used, s - NW + 1)
                    dve.tensor_scalar(weight_bits[:, s % NW, :], ps[:, L1[s][2] % ROUND, :], 0.0, None, ALU.max)\
                       .then_inc(weight_dve, 1)
                c = ends_chunk(s - LAG)
                if c is not None:
                    dve.wait_ge(count_ready, c + 1)
                    dve.tensor_scalar(rdeg[:, c * CH:(c + 1) * CH], ps[:, c % ROUND, :], -1.0 / P, 1.0, ALU.mult,
                                      ALU.max).then_inc(deg_read, 1)
                if s < len(L1) and s % 2 == 1 and L1[s][0] == 1:
                    w = ROUND * CH // (len(L1) // 4)
                    at = (s - len(L1) // 2) // 2 * w
                    dve.wait_ge(deg_read, ROUND)
                    dve.reciprocal(rdeg[:, at:at + w], rdeg[:, at:at + w]).then_inc(deg_ready, 1)
            for layer, pairs in ((1, pairs_b), (2, pairs_a)):
                for c in BY_DVE[layer]:
                    dve.wait_ge(y_copied[layer], c + 1)
                    node_update(dve, do, layer, c, ysb[:, c % 4], st[:, :, 0:CT], tmp_v, pairs, node_dve[layer])
                if layer == 1:
                    dve.wait_ge(deg_read, C)
                    dve.reciprocal(rdeg[:, ROUND * CH:C * CH], rdeg[:, ROUND * CH:C * CH]).then_inc(deg_ready, 1)

            for c in range(C + 1):
                if c < C:
                    dve.wait_ge(deg_ready, len(L1) // 4 + 1)
                    dve.wait_ge(sum_ready[3], c + 1)
                    if c == 0:
                        dve.wait_ge(y_ready[2], C)
                    if c >= 4:
                        dve.wait_ge(y_ready[3], c - 3)
                    dve.tensor_tensor(sums[:, c % 4, :], ps[:, c % OPEN, :], rdeg[:, c * CH:(c + 1) * CH], ALU.mult)\
                       .then_inc(sum_copied[3], 1)
                if c >= 1:
                    m = c - 1
                    dve.wait_ge(y_ready[3], m + 1)
                    X = x[:, chunk_tiles(m), :]
                    dve.scalar_tensor_tensor(X, ps[:, 7, 0:CT * D].rearrange("p (t d) -> p t d", d=D), 0.0, X,
                                             ALU.max, ALU.add).then_inc(out_ready, 1)


def kernel(**inputs):
    import numpy as np
    import concourse.bacc as bacc
    from concourse.bass_utils import run_bass_kernel_spmd

    a = {k: np.asarray(v) for k, v in inputs.items()}
    N, D = a["x"].shape
    T, C = N // 128, 8

    consts = np.zeros((128, NC_), np.float32)
    consts[:, 0:128] = np.eye(128)
    consts[:, 128:192] = np.concatenate([np.eye(D), np.eye(D) * 2.0 ** -11])
    j = np.arange(128)
    rank = 128.0 * (100.0 * np.eye(128) - (j[:, None] > j[None, :]))
    consts[:, 192:256] = np.concatenate([np.eye(D)] * 2)
    consts[:, 256] = np.where(j < D, 2.0 ** 27, 2.0 ** 16)
    consts[:, 257] = np.where(j < D, 1.0, 2.0 ** -11)

    def twice(w):
        both = np.zeros((2 * w.shape[0], 2 * w.shape[1]), w.dtype)
        both[:w.shape[0], :w.shape[1]] = w
        both[w.shape[0]:, w.shape[1]:] = w
        return both

    W3 = a["L3_gnn_W"]
    arrays = {
        "x_in": np.ascontiguousarray(a["x"]),
        "adj_in": np.ascontiguousarray(
            a["adj"].T.reshape(T, 128, C, N // C).transpose(1, 2, 0, 3)).reshape(128, C, T * (N // C)),
        "w0_in": twice(a["L0_gnn_W"].T),
        "wqk_in": twice(np.concatenate([a["L0_gnn_Wq"].T, a["L0_gnn_Wk"].T], axis=1)),
        "params_in": np.concatenate([np.tile(np.concatenate([a["L0_gnn_b"], a["L0_gnn_bq"], a["L0_gnn_bk"]]), (3, 1)),
                                     np.array([[0, 0], [-1, 0], [-1, -1]], np.float32),
                                     np.tile(np.concatenate([np.stack([a[k] for k in (
                                         "L0_gnn_scale", "L0_gnn_scale_q", "L0_gnn_scale_k", "L0_gnn_att_bias",
                                         "L0_gnn_att_scale")]), a["L1_gnn_bias"]]), (3, 1))], axis=1),
        "w1_in": np.concatenate([a["L1_gnn_weight"]] * 2),
        "w3h_in": twice(W3[:, :D].T),
        "w3n_in": np.concatenate([W3[:, D:].T] * 2),
        "consts_in": consts,
        "rank_in": np.concatenate([rank, -128.0 - rank], axis=1).astype(np.float32),
    }
    nc = bacc.Bacc("TRN2", target_bir_lowering=False, num_devices=1)
    args = [nc.dram_tensor(k, v.shape, mybir.dt.from_np(v.dtype), kind="ExternalInput").ap()
            for k, v in arrays.items()]
    out = nc.dram_tensor("out", (N, D), F32, kind="ExternalOutput").ap()
    gnn_program(nc, *args, out)
    r = run_bass_kernel_spmd(nc, [arrays], core_ids=[0])
    return r.results[0]["out"]
```
